# Optimizing a Trainium2 kernel written in Bass

```python
import numpy as np
import jax
import jax.numpy as jnp

def _softmax(x, axis=-1):
    return jax.nn.softmax(x, axis=axis)

def _gelu(x):
    return jax.nn.gelu(x, approximate=True)

def _silu(x):
    return jax.nn.silu(x)

def _sigmoid(x):
    return jax.nn.sigmoid(x)

def _layernorm(x, axis=-1, eps=1e-05):
    m = jnp.mean(x, axis=axis, keepdims=True)
    v = jnp.var(x, axis=axis, keepdims=True)
    return (x - m) / jnp.sqrt(v + eps)

def _scatter_add(tgt, idx, src, axis=0):
    return tgt.at[idx].add(src)

def _segment_sum(src, seg, n):
    return jax.ops.segment_sum(src, seg, n)
kernel_name = 'mk_gnn_ffn_d1_gnn_r8_159abd'

def setup_inputs(seed: int=0):
    np.random.seed(seed)
    _w = jnp.asarray

    def _rec_inputs():
        import jax
        import jax.numpy as jnp
        _gk = jax.random.key(seed)
        x = -0.0003713 + 1 * jax.random.normal(jax.random.fold_in(_gk, 1), (6250, 256), jnp.float32)
        src = jax.random.randint(jax.random.fold_in(_gk, 2), (200000,), 0, 6250, jnp.int32)
        dst = jax.random.randint(jax.random.fold_in(_gk, 3), (200000,), 0, 6250, jnp.int32)
        _o = jnp.argsort(dst, stable=True)
        src = src[_o]
        dst = dst[_o]
        return (x, src, dst)
    x, src, dst = _rec_inputs()

    def _L0_gnn_setup():
        import jax, jax.numpy as jnp
        import numpy as np
        N_NODES = 6250
        N_EDGES = 100000
        DIM = 256
        N_LAYERS = 3
        LN_EPS = 1e-05

        def _gcn_norm(edge_index, n_nodes, dtype):
            row, col = (edge_index[0], edge_index[1])
            loop = jnp.arange(n_nodes, dtype=edge_index.dtype)
            row = jnp.concatenate([row, loop])
            col = jnp.concatenate([col, loop])
            deg = jax.ops.segment_sum(jnp.ones(row.shape[0], dtype=dtype), col, num_segments=n_nodes)
            dinv = jnp.where(deg > 0, jax.lax.rsqrt(deg), 0.0)
            norm = dinv[row] * dinv[col]
            return (row, col, norm)
        key = jax.random.key(seed)
        ks = jax.random.split(key, 6)
        x = jax.random.normal(ks[0], (N_NODES, DIM), dtype=jnp.float32)
        edge_index = jax.random.randint(ks[1], (2, N_EDGES), 0, N_NODES, dtype=jnp.int64)
        W = jax.random.normal(ks[2], (N_LAYERS, DIM, DIM), dtype=jnp.float32) * (1.0 / np.sqrt(DIM))
        b = jax.random.normal(ks[3], (N_LAYERS, DIM), dtype=jnp.float32) * 0.02
        gamma = jnp.ones((N_LAYERS, DIM), dtype=jnp.float32)
        beta = jnp.zeros((N_LAYERS, DIM), dtype=jnp.float32)
        return {'x': x, 'W': W, 'b': b, 'gamma': gamma, 'beta': beta, 'edge_index': edge_index}
    _L0_gnn_all = _L0_gnn_setup()
    _L0_gnn_in = {k: v for k, v in _L0_gnn_all.items() if k in ('W', 'b', 'gamma', 'beta')}
    del _L0_gnn_all

    def _L0_ffn_setup():
        import jax, jax.numpy as jnp
        import numpy as np
        C = 256
        EPS = 1e-05
        N_ITERS = 30

        def _layernorm(x, w, bias):
            mu = jnp.mean(x, axis=-1, keepdims=True)
            var = jnp.mean(jnp.square(x - mu), axis=-1, keepdims=True)
            return (x - mu) * jax.lax.rsqrt(var + EPS) * w + bias
        key = jax.random.key(seed)
        kx, kw, kb, klw, klb = jax.random.split(key, 5)
        x = jax.random.normal(kx, (8, 256, C), dtype=jnp.float32)
        bound = 1.0 / np.sqrt(C)
        W = jax.random.uniform(kw, (C, C), minval=-bound, maxval=bound, dtype=jnp.float32)
        b = jax.random.uniform(kb, (C,), minval=-bound, maxval=bound, dtype=jnp.float32)
        ln_w = jnp.ones((C,), dtype=jnp.float32)
        ln_b = jnp.zeros((C,), dtype=jnp.float32)
        return {'x': x, 'ln_w': ln_w, 'ln_b': ln_b, 'W': W, 'b': b}
    _L0_ffn_all = _L0_ffn_setup()
    _L0_ffn_in = {k: v for k, v in _L0_ffn_all.items() if k in ('ln_w', 'ln_b', 'W', 'b')}
    del _L0_ffn_all
    return {'x': x, 'src': src, 'dst': dst, 'L0_gnn_W': _L0_gnn_in['W'], 'L0_gnn_b': _L0_gnn_in['b'], 'L0_gnn_gamma': _L0_gnn_in['gamma'], 'L0_gnn_beta': _L0_gnn_in['beta'], 'L0_ffn_ln_w': _L0_ffn_in['ln_w'], 'L0_ffn_ln_b': _L0_ffn_in['ln_b'], 'L0_ffn_W': _L0_ffn_in['W'], 'L0_ffn_b': _L0_ffn_in['b']}

def reference(x, src, dst, L0_gnn_W, L0_gnn_b, L0_gnn_gamma, L0_gnn_beta, L0_ffn_ln_w, L0_ffn_ln_b, L0_ffn_W, L0_ffn_b):
    import jax
    import jax.numpy as jnp

    def _L0_gnn_ref(x, W, b, gamma, beta, edge_index):
        import jax, jax.numpy as jnp
        import numpy as np
        N_NODES = 6250
        N_EDGES = 100000
        DIM = 256
        N_LAYERS = 3
        LN_EPS = 1e-05

        def _gcn_norm(edge_index, n_nodes, dtype):
            row, col = (edge_index[0], edge_index[1])
            loop = jnp.arange(n_nodes, dtype=edge_index.dtype)
            row = jnp.concatenate([row, loop])
            col = jnp.concatenate([col, loop])
            deg = jax.ops.segment_sum(jnp.ones(row.shape[0], dtype=dtype), col, num_segments=n_nodes)
            dinv = jnp.where(deg > 0, jax.lax.rsqrt(deg), 0.0)
            norm = dinv[row] * dinv[col]
            return (row, col, norm)
        n = x.shape[0]
        row, col, norm = _gcn_norm(edge_index, n, x.dtype)
        for i in range(N_LAYERS):
            h = x @ W[i]
            msg = h[row] * norm[:, None]
            h = jax.ops.segment_sum(msg, col, num_segments=n) + b[i]
            mu = jnp.mean(h, axis=-1, keepdims=True)
            var = jnp.mean((h - mu) ** 2, axis=-1, keepdims=True)
            h = (h - mu) * jax.lax.rsqrt(var + LN_EPS) * gamma[i] + beta[i]
            x = jax.nn.relu(h)
        return x

    def _L0_ffn_ref(x, ln_w, ln_b, W, b):
        import jax, jax.numpy as jnp
        import numpy as np
        C = 256
        EPS = 1e-05
        N_ITERS = 30

        def _layernorm(x, w, bias):
            mu = jnp.mean(x, axis=-1, keepdims=True)
            var = jnp.mean(jnp.square(x - mu), axis=-1, keepdims=True)
            return (x - mu) * jax.lax.rsqrt(var + EPS) * w + bias

        def step(h, _):
            h = h + 0.01 * jnp.tanh(h)
            h = h * jax.nn.sigmoid(h)
            h = _layernorm(h, ln_w, ln_b)
            h = jnp.einsum('bsc,dc->bsd', h, W) + b
            return (h, None)
        x, _ = jax.lax.scan(step, x, None, length=N_ITERS)
        return x
    edge_index = jnp.stack([src, dst])
    x = x + _L0_gnn_ref(_layernorm(x, axis=-1), L0_gnn_W, L0_gnn_b, L0_gnn_gamma, L0_gnn_beta, edge_index)
    x = x + _L0_ffn_ref(_layernorm(x, axis=-1)[None], L0_ffn_ln_w, L0_ffn_ln_b, L0_ffn_W, L0_ffn_b)[0]
    return x

_drawn_inputs = setup_inputs


def setup_inputs(seed=0):
    import zlib

    import numpy as np

    out = dict(_drawn_inputs(seed))
    spreads = {'L0_gnn_gamma': (1.0, 0.2),
     'L0_gnn_beta': (0.0, 0.1),
     'L0_ffn_ln_w': (1.0, 0.2),
     'L0_ffn_ln_b': (0.0, 0.1)}
    factors = {}
    for name, (base, spread) in spreads.items():
        noise = np.random.default_rng([zlib.crc32(name.encode()), seed]).standard_normal(out[name].shape)
        drawn = base * np.exp(spread * noise) if base else spread * noise
        out[name] = jnp.asarray(drawn.astype(out[name].dtype))
    for name, factor in factors.items():
        out[name] = (out[name] * factor).astype(out[name].dtype)
    return out
```

```python
import concourse.bass as bass
from concourse import mybir
from contextlib import ExitStack

P = 128
F32 = mybir.dt.float32
BF16 = mybir.dt.bfloat16
I32 = mybir.dt.int32
ALU = mybir.AluOpType
ACT = mybir.ActivationFunctionType
AX = mybir.AxisListType

EPS = 1e-5
RES_SCALE = 0.01
N_ITERS = 30
NO_NODE = 1 << 20

TS = 7


def pipeline(eng, slots, depth, unroll, stage):
    assert depth % unroll == 0
    body = (slots - depth) // unroll
    for k in range(depth):
        stage(k, k % unroll)
    with eng.Fori(depth, depth + body * unroll, unroll) as k0:
        for u in range(unroll):
            stage(k0 + u, u)
    for k in range(depth + body * unroll, slots + depth):
        stage(k, k % unroll)


def build_gnn_ffn(nc, x, src, dst, gnn_w, gnn_b, gnn_gamma, gnn_beta, ffn_ln_w, ffn_ln_b, ffn_w, ffn_b, out):
    N, D = x.shape
    E = src.shape[0]
    L = gnn_w.shape[0]
    KC = D // P
    T = -(-N // P)
    LAST = N - (T - 1) * P
    CB = -(-E // (P * P))
    CH = CB * P
    FULL_CB = E // (P * P)
    FULL_ROWS = (E - FULL_CB * P * P) // P
    REST = E % P
    G = T // TS
    assert G * TS == T

    root = ExitStack()
    with root:
        def sem(name):
            return root.enter_context(nc.semaphore(name))

        def sb(stack, name, shape, dt=F32):
            return stack.enter_context(nc.sbuf_tensor(name, shape, dt))

        def ps(stack, name, shape, dt=F32):
            return stack.enter_context(nc.psum_tensor(name, shape, dt))

        def dram(name, shape, dt):
            return nc.dram_tensor(name, shape, dt, kind="Internal").ap()

        resid = sb(root, "resid", [P, T, D])
        state = sb(root, "state", [P, T, D])
        mv = sb(root, "mv", [P, T, 2])
        rstd = sb(root, "rstd", [P, T])
        dinv = sb(root, "dinv", [P, T])
        neg_half = sb(root, "neg_half", [P, T])
        eps_tile = sb(root, "eps_tile", [P, TS])
        iota_row = sb(root, "iota_row", [P, P])
        iota_bf = sb(root, "iota_bf", [P, P], BF16)
        iota_part = sb(root, "iota_part", [P, 1])
        ident = sb(root, "ident", [P, P])
        w_gnn = sb(root, "w_gnn", [P, L, KC, D])
        rows3 = sb(root, "rows3", [P, L, 3, D])
        w_scan = sb(root, "w_scan", [P, KC, D])
        b_scan = sb(root, "b_scan", [P, D])

        h_tab = dram("h_tab", [T * P, D], F32)
        lo_row = dram("chunk_least", [CB, P], F32)
        hi_row = dram("chunk_most", [CB, P], F32)
        range_row = dram("range_row", [T, 2], F32)

        edge_stack = root.enter_context(ExitStack())
        dst_col = sb(edge_stack, "dst_col", [P, CH])
        src_col = sb(edge_stack, "src_col", [P, CH], I32)
        tab = sb(edge_stack, "tab", [1, T, 4], I32)

        x_loaded = sem("x_loaded")
        edges_loaded = sem("edges_loaded")
        params_loaded = sem("params_loaded")
        pad_set = sem("pad_set")
        const_set = sem("const_set")
        col_ready = sem("col_ready")
        blk_done = sem("blk_done")
        flt_done = sem("flt_done")
        minmax_done = sem("minmax_done")
        rows_stored = sem("rows_stored")

        with ExitStack() as ph:
            dst_nat = sb(ph, "dst_nat", [P, CB, P], I32)
            src_nat = sb(ph, "src_nat", [P, CB, P], I32)
            dst_f = sb(ph, "dst_f", [P, CB, P])
            src_f = sb(ph, "src_f", [P, CB, P])
            tmin = sb(ph, "tmin", [P, CB])
            tmax = sb(ph, "tmax", [P, CB])
            tr = ps(ph, "tr", [P, 4, 512])
            tr2 = ps(ph, "tr2", [P, 4, 512])
            with nc.Block() as block:
                @block.sync
                def _(sp):
                    n_full = FULL_CB * P * P
                    n_rows = n_full + FULL_ROWS * P
                    sp.wait_ge(pad_set, 2)
                    for nat, e in ((dst_nat, dst), (src_nat, src)):
                        sp.dma_start(nat[:, 0:FULL_CB, :],
                                     e[0:n_full].rearrange("(b p e) -> p b e", p=P, e=P)).then_inc(edges_loaded, 16)
                        sp.dma_start(nat[0:FULL_ROWS, FULL_CB, :],
                                     e[n_full:n_rows].rearrange("(p e) -> p e", e=P)).then_inc(edges_loaded, 16)
                        sp.dma_start(nat[FULL_ROWS:FULL_ROWS + 1, FULL_CB, 0:REST],
                                     e[n_rows:E].rearrange("(p e) -> p e", p=1)).then_inc(edges_loaded, 16)
                    sp.dma_start(resid[:, 0:T - 1, :],
                                 x[0:(T - 1) * P, :].rearrange("(t p) d -> p t d", p=P)).then_inc(x_loaded, 16)
                    sp.wait_ge(pad_set, 3)
                    sp.dma_start(resid[0:LAST, T - 1, :], x[(T - 1) * P:N, :]).then_inc(x_loaded, 16)

                @block.scalar
                def _(act):
                    for i in range(L):
                        act.dma_start(w_gnn[:, i, :, :],
                                      gnn_w[i, :, :].rearrange("(k p) d -> p k d", p=P)).then_inc(params_loaded, 16)
                        for j, v in enumerate((gnn_b, gnn_gamma, gnn_beta)):
                            act.dma_start(rows3[:, i, j, :],
                                          v[i:i + 1, :].partition_broadcast(P)).then_inc(params_loaded, 16)
                    act.wait_ge(params_loaded, 16 * 4 * L)

                @block.gpsimd
                def _(pool):
                    nc.gpsimd.iota(iota_row[:, :], [[1, P]], base=0, channel_multiplier=0,
                                   allow_small_or_imprecise_dtypes=True)
                    nc.gpsimd.iota(iota_bf[:, :], [[1, P]], base=0, channel_multiplier=0,
                                   allow_small_or_imprecise_dtypes=True)
                    nc.gpsimd.iota(iota_part[:, :], [[0, 1]], base=0, channel_multiplier=1,
                                   allow_small_or_imprecise_dtypes=True)
                    nc.gpsimd.memset(neg_half[:, :], -0.5)
                    nc.gpsimd.memset(eps_tile[:, :], EPS)
                    nc.gpsimd.memset(ident[:, :], 0.0).then_inc(const_set, 1)
                    pool.wait_ge(const_set, 1)
                    nc.gpsimd.affine_select(out=ident[:, :], in_=ident[:, :], compare_op=ALU.not_equal, fill=1.0,
                                            base=0, pattern=[[-1, P]], channel_multiplier=1).then_inc(const_set, 1)

                @block.vector
                def _(dve):
                    nc.vector.memset(dst_nat[:, FULL_CB, :], NO_NODE).then_inc(pad_set, 1)
                    nc.vector.memset(src_nat[:, FULL_CB, :], 0).then_inc(pad_set, 1)
                    nc.vector.memset(resid[:, T - 1, :], 0.0).then_inc(pad_set, 1)
                    dve.wait_ge(edges_loaded, 96)
                    nc.vector.tensor_copy(dst_f[:, :, :], dst_nat[:, :, :]).then_inc(flt_done, 1)
                    nc.vector.tensor_copy(src_f[:, :, :], src_nat[:, :, :]).then_inc(flt_done, 1)
                    dve.wait_ge(flt_done, 1)
                    nc.vector.tensor_reduce(tmin[:, :], dst_f[:, :, :], AX.X, ALU.min).then_inc(minmax_done, 1)
                    nc.vector.tensor_reduce(tmax[:, :], dst_f[:, :, :], AX.X, ALU.max).then_inc(minmax_done, 1)
                    for b in range(CB):
                        dve.wait_ge(col_ready, 2 * b + 1)
                        nc.vector.tensor_copy(dst_col[:, b * P:(b + 1) * P], tr[:, b % 4, 0:P]).then_inc(blk_done, 1)
                        dve.wait_ge(col_ready, 2 * b + 2)
                        nc.vector.tensor_copy(src_col[:, b * P:(b + 1) * P], tr2[:, b % 4, 0:P]).then_inc(blk_done, 1)

                @block.tensor
                def _(pe):
                    pe.wait_ge(const_set, 2)
                    pe.wait_ge(flt_done, 2)
                    for b in range(CB):
                        if b >= 4:
                            pe.wait_ge(blk_done, 2 * (b - 4) + 2)
                        nc.tensor.transpose(tr[:, b % 4, 0:P], dst_f[:, b, :], ident[:, :]).then_inc(col_ready, 1)
                        nc.tensor.transpose(tr2[:, b % 4, 0:P], src_f[:, b, :], ident[:, :]).then_inc(col_ready, 1)

            with nc.Block() as block:
                @block.sync
                def _(sp):
                    with nc.allow_non_contiguous_dma(reason="one small table"):
                        sp.dma_start(lo_row.rearrange("b p -> p b"), tmin[:, :]).then_inc(rows_stored, 16)
                        sp.dma_start(hi_row.rearrange("b p -> p b"), tmax[:, :]).then_inc(rows_stored, 16)
                    sp.wait_ge(rows_stored, 32)
                    sp.wait_ge(x_loaded, 32)

        split_done = sem("split_done")
        onehots_ready = sem("onehots_ready")
        onehots_used = sem("onehots_used")
        deg_opened = sem("deg_opened")
        deg_done = sem("deg_done")
        dinv_ready = sem("dinv_ready")
        U = 8
        with ExitStack() as ph:
            dst_i = sb(ph, "dst_i", [P, CH], I32)
            part_i = sb(ph, "part_i", [P, 2, CH], I32)
            part_f = sb(ph, "part_f", [P, 2, CH])
            zero_b = sb(ph, "zero_b", [P, P], BF16)
            hot_row = sb(ph, "hot_row", [P, U, P], BF16)
            hot_tile = sb(ph, "hot_tile", [P, U, T], BF16)
            deg1 = sb(ph, "deg1", [P, T])
            deg_ps = ps(ph, "deg_ps", [P, T])
            with nc.Block() as block:
                @block.vector
                def _(dve):
                    nc.vector.memset(zero_b[:, :], 0.0).then_inc(split_done, 1)
                    nc.vector.tensor_copy(dst_i[:, :], dst_col[:, :]).then_inc(split_done, 1)
                    dve.wait_ge(split_done, 2)
                    nc.vector.tensor_scalar(part_i[:, 0, :], dst_i[:, :], P - 1, None, ALU.bitwise_and).then_inc(split_done, 1)
                    nc.vector.tensor_scalar(part_i[:, 1, :], dst_i[:, :], 7, None, ALU.arith_shift_right).then_inc(split_done, 1)
                    dve.wait_ge(split_done, 4)
                    nc.vector.tensor_copy(part_f[:, :, :], part_i[:, :, :]).then_inc(split_done, 1)
                    dve.wait_ge(split_done, 5)

                    def chunks(it, first):
                        for u in range(U):
                            k = it * U + u
                            if not first:
                                dve.wait_ge(onehots_used, (it - 1) * U + u + 1)
                            nc.vector.tensor_scalar(hot_row[:, u, :], iota_bf[:, :], part_f[:, 0, bass.ds(k, 1)],
                                                    None, ALU.is_equal)
                            nc.vector.tensor_scalar(hot_tile[:, u, :], iota_bf[:, 0:T], part_f[:, 1, bass.ds(k, 1)],
                                                    None, ALU.is_equal).then_inc(onehots_ready, 1)
                    chunks(0, True)
                    with dve.Fori(1, CH // U) as it:
                        chunks(it, False)
                    dve.wait_ge(deg_done, 1)
                    nc.vector.tensor_scalar(deg1[:, :], deg_ps[:, :], 1.0, None, ALU.add).then_inc(split_done, 1)

                @block.tensor
                def _(pe):
                    pe.wait_ge(split_done, 1)
                    nc.tensor.matmul(deg_ps[:, :], zero_b[:, :], zero_b[:, 0:T], start=True, stop=False)
                    with pe.Fori(0, CH // U) as it:
                        for u in range(U):
                            pe.wait_ge(onehots_ready, it * U + u + 1)
                            nc.tensor.matmul(deg_ps[:, :], hot_row[:, u, :], hot_tile[:, u, :], start=False,
                                             stop=False).then_inc(onehots_used, 1)
                    nc.tensor.matmul(deg_ps[:, :], zero_b[:, :], zero_b[:, 0:T], start=False, stop=True).then_inc(deg_done, 1)

                @block.gpsimd
                def _(pool):
                    pool.wait_ge(split_done, 6)
                    nc.gpsimd.tensor_tensor(dinv[:, :], deg1[:, :], neg_half[:, :], ALU.pow).then_inc(dinv_ready, 1)

        rows_loaded = sem("rows_loaded")
        rng = sem("rng")
        tab_stored = sem("tab_stored")
        tab_loaded = sem("tab_loaded")
        cnt_ready = sem("cnt_ready")
        kdown_set = sem("kdown_set")
        with ExitStack() as ph:
            least = sb(ph, "least", [P, CH])
            most = sb(ph, "most", [P, CH])
            kup = sb(ph, "kup", [P, CH])
            kdown = sb(ph, "kdown", [P, CH])
            picked = sb(ph, "picked", [P, 2, CH])
            thr = sb(ph, "thr", [P, 2])
            ends = sb(ph, "ends", [P, 4])
            pair = sb(ph, "pair", [P, 2])
            line = sb(ph, "line", [1, T, 2])
            cum = sb(ph, "cum", [1, T])
            zline = sb(ph, "zline", [1, T])
            tab_f = sb(ph, "tab_f", [1, T, 4])
            with nc.Block() as block:
                @block.sync
                def _(sp):
                    sp.dma_start(least[:, :], lo_row.rearrange("b p -> (b p)").partition_broadcast(P)).then_inc(rows_loaded, 16)
                    sp.dma_start(most[:, :], hi_row.rearrange("b p -> (b p)").partition_broadcast(P)).then_inc(rows_loaded, 16)
                    sp.wait_ge(cnt_ready, 1)
                    sp.dma_start(range_row[:, :], pair[0:T, :]).then_inc(tab_stored, 16)
                    sp.wait_ge(tab_stored, 16)
                    sp.dma_start(line[:, :, :], range_row.rearrange("(a t) c -> a t c", a=1)).then_inc(tab_loaded, 16)

                @block.gpsimd
                def _(pool):
                    nc.gpsimd.iota(kup[:, :], [[1, CH]], base=1, channel_multiplier=0,
                                   allow_small_or_imprecise_dtypes=True)
                    nc.gpsimd.iota(kdown[:, :], [[-1, CH]], base=CH, channel_multiplier=0,
                                   allow_small_or_imprecise_dtypes=True).then_inc(kdown_set, 1)

                @block.vector
                def _(dve):
                    n = [0]

                    def link(ins):
                        n[0] += 1
                        ins.then_inc(rng, 1)
                        dve.wait_ge(rng, n[0])
                    v = nc.vector
                    v.tensor_scalar(thr[:, 0:1], iota_part[:, :], float(P), None, ALU.mult)
                    link(v.tensor_scalar(thr[:, 1:2], iota_part[:, :], float(P), float(P - 1), ALU.mult, ALU.add))
                    dve.wait_ge(rows_loaded, 32)
                    dve.wait_ge(kdown_set, 1)
                    link(v.scalar_tensor_tensor(picked[:, 0, :], most[:, :], thr[:, 0:1], kdown[:, :], ALU.is_ge, ALU.mult))
                    link(v.scalar_tensor_tensor(picked[:, 1, :], least[:, :], thr[:, 1:2], kup[:, :], ALU.is_le, ALU.mult))
                    link(v.tensor_reduce(ends[:, 0:2], picked[:, :, :], AX.X, ALU.max))
                    link(v.tensor_scalar(pair[:, 0:1], ends[:, 0:1], -1.0, float(CH), ALU.mult, ALU.add))
                    link(v.tensor_tensor(ends[:, 2:3], ends[:, 1:2], pair[:, 0:1], ALU.subtract))
                    v.tensor_scalar(pair[:, 1:2], ends[:, 2:3], 1.0, None, ALU.max).then_inc(cnt_ready, 1)
                    link(v.memset(zline[:, :], 0.0))
                    dve.wait_ge(tab_loaded, 16)
                    link(v.tensor_tensor_scan(cum[:, :], line[:, :, 1], zline[:, :], 0.0, ALU.add, ALU.add))
                    link(v.tensor_tensor(tab_f[:, :, 0], cum[:, :], line[:, :, 1], ALU.subtract))
                    v.tensor_copy(tab_f[:, :, 1], line[:, :, 1])
                    v.tensor_copy(tab_f[:, :, 3], line[:, :, 1])
                    link(v.tensor_copy(tab_f[:, :, 2], line[:, :, 0]))
                    link(v.tensor_copy(tab[:, :, :], tab_f[:, :, :]))

        def row_stats(i, name):
            made, stats, small, ready = (sem(f"{name}_{s}") for s in ("made", "stats", "small", "ready"))
            frm = state if i > 0 else resid
            with ExitStack() as ph:
                st = sb(ph, f"{name}_st", [P, T, 6])
                half = sb(ph, f"{name}_half", [P, T])
                with nc.Block() as block:
                    @block.vector
                    def _(dve):
                        v = nc.vector
                        if i > 0:
                            with dve.Fori(0, T) as t:
                                row = state[:, bass.ds(t, 1), :].rearrange("p a d -> p (a d)")
                                v.scalar_tensor_tensor(row, row, dinv[:, bass.ds(t, 1)], rows3[:, i - 1, 0, :],
                                                       ALU.mult, ALU.add).then_inc(made, 1)
                            dve.wait_ge(made, T)
                        with dve.Fori(0, T) as t:
                            v.bn_stats(st[:, bass.ds(t, 1), :].rearrange("p a d -> p (a d)"),
                                       frm[:, bass.ds(t, 1), :].rearrange("p a d -> p (a d)")).then_inc(stats, 1)
                        dve.wait_ge(stats, T)
                        v.tensor_tensor(mv[:, :, 0], st[:, :, 1], st[:, :, 4], ALU.add).then_inc(small, 1)
                        v.tensor_tensor(half[:, :], st[:, :, 1], st[:, :, 4], ALU.subtract).then_inc(small, 1)
                        v.tensor_tensor(mv[:, :, 1], st[:, :, 2], st[:, :, 5], ALU.add).then_inc(small, 1)
                        dve.wait_ge(small, 3)
                        v.tensor_scalar(mv[:, :, 0], mv[:, :, 0], 0.5, None, ALU.mult).then_inc(small, 1)
                        v.scalar_tensor_tensor(half[:, :], half[:, :], 0.25, half[:, :], ALU.mult, ALU.mult).then_inc(small, 1)
                        v.tensor_scalar(mv[:, :, 1], mv[:, :, 1], 1.0 / D, EPS, ALU.mult, ALU.add).then_inc(small, 1)
                        dve.wait_ge(small, 6)
                        v.tensor_tensor(mv[:, :, 1], mv[:, :, 1], half[:, :], ALU.add).then_inc(small, 1)

                    @block.gpsimd
                    def _(pool):
                        pool.wait_ge(small, 7)
                        nc.gpsimd.tensor_tensor(rstd[:, :], mv[:, :, 1], neg_half[:, :], ALU.pow).then_inc(ready, 1)

        def layer_input(dve, i, t, xr, dch, base):
            v = nc.vector
            tt = bass.ds(t, 1)
            frm = (resid if i == 0 else state)[:, tt, :].rearrange("p a d -> p (a d)")
            v.tensor_scalar(xr, frm, mv[:, tt, 0:1].rearrange("p a c -> p (a c)"), rstd[:, tt],
                            ALU.subtract, ALU.mult).then_inc(dch, 1)
            if i > 0:
                dve.wait_ge(dch, base + 1)
                v.tensor_tensor(xr, xr, rows3[:, i - 1, 1, :], ALU.mult).then_inc(dch, 1)
                dve.wait_ge(dch, base + 2)
                v.tensor_tensor(xr, xr, rows3[:, i - 1, 2, :], ALU.add).then_inc(dch, 1)
                dve.wait_ge(dch, base + 3)
                v.tensor_scalar(xr, xr, 0.0, None, ALU.max).then_inc(dch, 1)

        def layer_product(i):
            nm = f"l{i}p"
            x_made, x_turned, xt_copied, prod, h_made, h_stored, dch = (
                sem(f"{nm}_{s}") for s in ("x_made", "x_turned", "xt_copied", "prod", "h_made", "h_stored", "dch"))
            per = 1 if i == 0 else 4
            with ExitStack() as ph:
                xr = sb(ph, f"{nm}_xr", [P, 2, D])
                xt = sb(ph, f"{nm}_xt", [P, 2, KC, P])
                xt_ps = ps(ph, f"{nm}_xt_ps", [P, 2, 512])
                h_ps = ps(ph, f"{nm}_h_ps", [P, 2, 512])
                with nc.Block() as block:
                    @block.vector
                    def _(dve):
                        def stage(k, u):
                            static = isinstance(k, int)
                            if not static or k < T:
                                if not static or k >= 2:
                                    dve.wait_ge(x_turned, k - 1)
                                layer_input(dve, i, k, xr[:, u, :], dch, k * per)
                                dve.wait_ge(dch, (k + 1) * per)
                                dve.sem_inc(x_made, 1)
                            if not static or 1 <= k <= T:
                                t = k - 1
                                dve.wait_ge(prod, t + 1)
                                nc.vector.tensor_scalar(state[:, bass.ds(t, 1), :].rearrange("p a d -> p (a d)"),
                                                        h_ps[:, 1 - u, 0:D], dinv[:, bass.ds(t, 1)], None,
                                                        ALU.mult).then_inc(h_made, 1)
                        pipeline(dve, T, 2, 2, stage)

                    @block.tensor
                    def _(pe):
                        def stage(k, u):
                            static = isinstance(k, int)
                            if not static or k < T:
                                pe.wait_ge(x_made, k + 1)
                                if not static or k >= 2:
                                    pe.wait_ge(xt_copied, k - 1)
                                for c in range(KC):
                                    last = nc.tensor.transpose(xt_ps[:, u, c * P:(c + 1) * P],
                                                               xr[:, u, c * P:(c + 1) * P], ident[:, :])
                                last.then_inc(x_turned, 1)
                            if not static or 1 <= k <= T:
                                t = k - 1
                                pe.wait_ge(xt_copied, t + 1)
                                if not static or t >= 2:
                                    pe.wait_ge(h_made, t - 1)
                                for c in range(KC):
                                    last = nc.tensor.matmul(h_ps[:, 1 - u, 0:D], xt[:, 1 - u, c, :], w_gnn[:, i, c, :],
                                                            start=c == 0, stop=c == KC - 1)
                                last.then_inc(prod, 1)
                        pipeline(pe, T, 2, 2, stage)

                    @block.scalar
                    def _(act):
                        def copy(t, u, first):
                            act.wait_ge(x_turned, t + 1)
                            if not first:
                                act.wait_ge(prod, t - 1)
                            nc.scalar.activation(xt[:, u, :, :].rearrange("p c n -> p (c n)"), xt_ps[:, u, 0:D],
                                                 ACT.Copy).then_inc(xt_copied, 1)
                        copy(0, 0, True)
                        copy(1, 1, True)
                        with act.Fori(2, T - 1, 2) as t0:
                            copy(t0, 0, False)
                            copy(t0 + 1, 1, False)
                        copy(T - 1, 0, False)

                    @block.sync
                    def _(sp):
                        with sp.Fori(0, T) as t:
                            sp.wait_ge(h_made, t + 1)
                            sp.dma_start(h_tab[bass.ds(t * P, P), :],
                                         state[:, bass.ds(t, 1), :].rearrange("p a d -> p (a d)")).then_inc(h_stored, 16)
                        sp.wait_ge(h_stored, 16 * T)

        def gather_sum(i):
            nm = f"l{i}g"
            idx_ready, idx_seen, rows_ready, hot_ready, summed, free, iota_set = (
                sem(f"{nm}_{s}") for s in ("idx", "idx_seen", "rows", "hot", "summed", "free", "iota"))
            with ExitStack() as ph:
                idx = sb(ph, f"{nm}_idx", [P, 1], I32)
                rows = sb(ph, f"{nm}_rows", [P, D])
                hot = sb(ph, f"{nm}_hot", [P, P])
                tile_iota = sb(ph, f"{nm}_iota_t", [P, P])
                sum_ps = ps(ph, f"{nm}_ps", [P, D])

                def steps(eng, body):
                    with eng.Fori(0, T) as t:
                        s0 = eng.value_load(tab[0:1, bass.ds(t, 1), 0:1].rearrange("p a b -> p (a b)"), min_val=0, max_val=T * CH)
                        n = eng.value_load(tab[0:1, bass.ds(t, 1), 1:2].rearrange("p a b -> p (a b)"), min_val=1, max_val=CH)
                        k0 = eng.value_load(tab[0:1, bass.ds(t, 1), 2:3].rearrange("p a b -> p (a b)"), min_val=0, max_val=CH - 1)
                        with eng.Fori(0, n) as j:
                            body(t, s0 + j, k0 + j)

                with nc.Block() as block:
                    @block.gpsimd
                    def _(pool):
                        def body(t, s, k):
                            pool.wait_ge(free, s + 1)
                            nc.gpsimd.tensor_copy(idx[:, :], src_col[:, bass.ds(nc.s_assert_within(k, 0, CH - 1), 1)]).then_inc(idx_ready, 1)
                            pool.wait_ge(idx_ready, s + 1)
                            pool.sem_inc(idx_seen, 1)
                            nc.gpsimd.indirect_dma_start(rows[:, :], None, h_tab[:, :],
                                                         bass.IndirectOffsetOnAxis(idx[:, 0:1], 0)).then_inc(rows_ready, 16)
                        steps(pool, body)

                    @block.vector
                    def _(dve):
                        def body(t, s, k):
                            kk = nc.s_assert_within(k, 0, CH - 1)
                            nc.vector.tensor_scalar(hot[:, :], tile_iota[:, :], dst_col[:, bass.ds(kk, 1)], None,
                                                    ALU.is_equal).then_inc(hot_ready, 1)
                            dve.wait_ge(summed, s + 1)
                            st = state[:, bass.ds(t, 1), :].rearrange("p a d -> p (a d)")
                            nc.vector.tensor_tensor(st, sum_ps[:, :], st, ALU.add).then_inc(free, 1)
                            dve.wait_ge(free, s + 2)

                        dve.sem_inc(free, 1)
                        nc.vector.tensor_copy(tile_iota[:, :], iota_row[:, :]).then_inc(iota_set, 1)
                        dve.wait_ge(iota_set, 1)
                        with dve.Fori(0, T) as t:
                            s0 = dve.value_load(tab[0:1, bass.ds(t, 1), 0:1].rearrange("p a b -> p (a b)"), min_val=0, max_val=T * CH)
                            n = dve.value_load(tab[0:1, bass.ds(t, 1), 1:2].rearrange("p a b -> p (a b)"), min_val=1, max_val=CH)
                            k0 = dve.value_load(tab[0:1, bass.ds(t, 1), 2:3].rearrange("p a b -> p (a b)"), min_val=0, max_val=CH - 1)
                            with dve.Fori(0, n) as j:
                                body(t, s0 + j, k0 + j)
                            nc.vector.tensor_scalar(tile_iota[:, :], tile_iota[:, :], float(P), None, ALU.add).then_inc(iota_set, 1)
                            dve.wait_ge(iota_set, t + 2)

                    @block.tensor
                    def _(pe):
                        def body(t, s, k):
                            pe.wait_ge(rows_ready, (s + 1) * 16)
                            pe.wait_ge(hot_ready, s + 1)
                            pe.wait_ge(free, s + 1)
                            nc.tensor.matmul(sum_ps[:, :], hot[:, :], rows[:, :], start=True, stop=True).then_inc(summed, 1)
                        steps(pe, body)

        for i in range(L):
            row_stats(i, f"st{i}")
            layer_product(i)
            gather_sum(i)
        edge_stack.close()

        row_stats(L, "stl")
        fin = sem("fin")
        with ExitStack() as ph:
            xr = sb(ph, "fin_x", [P, D])
            with nc.Block() as block:
                @block.vector
                def _(dve):
                    with dve.Fori(0, T) as t:
                        layer_input(dve, L, t, xr[:, :], fin, t * 5)
                        dve.wait_ge(fin, t * 5 + 4)
                        r = resid[:, bass.ds(t, 1), :].rearrange("p a d -> p (a d)")
                        nc.vector.tensor_tensor(r, r, xr[:, :], ALU.add).then_inc(fin, 1)
                        dve.wait_ge(fin, t * 5 + 5)
        row_stats(0, "stx")
        with nc.Block() as block:
            @block.vector
            def _(dve):
                with dve.Fori(0, T) as t:
                    tt = bass.ds(t, 1)
                    nc.vector.tensor_scalar(state[:, tt, :].rearrange("p a d -> p (a d)"),
                                            resid[:, tt, :].rearrange("p a d -> p (a d)"),
                                            mv[:, tt, 0:1].rearrange("p a c -> p (a c)"), rstd[:, tt],
                                            ALU.subtract, ALU.mult)

        fw_loaded = sem("fw_loaded")
        fw_turned = sem("fw_turned")
        fw_dve = sem("fw_dve")
        fw_sum = sem("fw_sum")
        with ExitStack() as ph:
            w_nat = sb(ph, "w_nat", [P, KC, D])
            w_raw = sb(ph, "w_raw", [P, KC, D])
            w_scaled = sb(ph, "w_scaled", [P, KC, D])
            lnw = sb(ph, "lnw", [P, KC])
            lnb = sb(ph, "lnb", [P, KC])
            lnb_wide = sb(ph, "lnb_wide", [P, KC, P])
            mean_mat = sb(ph, "mean_mat", [P, P])
            fb = sb(ph, "fb", [P, D])
            wt_ps = ps(ph, "wt_ps", [P, KC, D])
            bias_ps = ps(ph, "bias_ps", [P, D])
            mean_ps = ps(ph, "mean_ps", [P, D])
            with nc.Block() as block:
                @block.sync
                def _(sp):
                    sp.dma_start(w_nat[:, :, :], ffn_w.rearrange("(k p) c -> p k c", p=P)).then_inc(fw_loaded, 16)
                    sp.dma_start(fb[:, :], ffn_b.partition_broadcast(P)).then_inc(fw_loaded, 16)
                    with nc.allow_non_contiguous_dma(reason="two vectors onto partitions"):
                        sp.dma_start(lnw[:, :], ffn_ln_w.rearrange("(k p) -> p k", p=P)).then_inc(fw_loaded, 16)
                        sp.dma_start(lnb[:, :], ffn_ln_b.rearrange("(k p) -> p k", p=P)).then_inc(fw_loaded, 16)

                @block.tensor
                def _(pe):
                    pe.wait_ge(fw_loaded, 64)
                    for c in range(KC):
                        for d in range(KC):
                            last = nc.tensor.transpose(wt_ps[:, c, d * P:(d + 1) * P], w_nat[:, d, c * P:(c + 1) * P], ident[:, :])
                    last.then_inc(fw_turned, 1)
                    pe.wait_ge(fw_dve, 3 + 2 * KC)
                    for c in range(KC):
                        nc.tensor.matmul(bias_ps[:, :], lnb_wide[:, c, :], w_raw[:, c, :], start=c == 0, stop=c == KC - 1)
                    for c in range(KC):
                        last = nc.tensor.matmul(mean_ps[:, :], mean_mat[:, :], w_scaled[:, c, :], start=c == 0, stop=c == KC - 1)
                    last.then_inc(fw_sum, 1)

                @block.vector
                def _(dve):
                    v = nc.vector
                    v.memset(mean_mat[:, :], 1.0 / D).then_inc(fw_dve, 1)
                    v.memset(lnb_wide[:, :, :], 1.0).then_inc(fw_dve, 1)
                    dve.wait_ge(fw_loaded, 64)
                    dve.wait_ge(fw_dve, 2)
                    dve.wait_ge(fw_turned, 1)
                    v.tensor_copy(w_raw[:, :, :], wt_ps[:, :, :]).then_inc(fw_dve, 1)
                    for c in range(KC):
                        v.tensor_scalar(lnb_wide[:, c, :], lnb_wide[:, c, :], lnb[:, c:c + 1], None, ALU.mult).then_inc(fw_dve, 1)
                        v.tensor_scalar(w_scaled[:, c, :], wt_ps[:, c, :], lnw[:, c:c + 1], None, ALU.mult).then_inc(fw_dve, 1)
                    dve.wait_ge(fw_dve, 3 + 2 * KC)
                    dve.wait_ge(fw_sum, 1)
                    for c in range(KC):
                        v.tensor_tensor(w_scan[:, c, :], w_scaled[:, c, :], mean_ps[:, :], ALU.subtract)
                    v.tensor_tensor(b_scan[:, :], fb[:, :], bias_ps[:, :], ALU.add)

        S = N_ITERS * G
        BANKS = -(-TS // 2)
        names = ("tanh_done", "h2_done", "sig_done", "z_done", "var_done", "rstd_done", "z_turned", "zt_copied",
                 "prod_done", "h_done", "var_ch", "eps_added")
        (tanh_done, h2_done, sig_done, z_done, var_done, rstd_done, z_turned, zt_copied, prod_done, h_done,
         var_ch, eps_added) = (sem(s) for s in names)
        with ExitStack() as ph:
            th = sb(ph, "th", [P, 2, TS, D])
            h2 = sb(ph, "h2", [P, 2, TS, D])
            sg = sb(ph, "sg", [P, 2, TS, D])
            z = sb(ph, "z", [P, 2, TS, D])
            zt = sb(ph, "zt", [P, 2, TS * 2, P])
            zst = sb(ph, "zst", [P, TS, 6])
            zhalf = sb(ph, "zhalf", [P, TS])
            zsum = sb(ph, "zsum", [P, TS])
            zeps = sb(ph, "zeps", [P, 2, TS])
            zvar = sb(ph, "zvar", [P, 2, TS])
            zrs = sb(ph, "zrs", [P, 2, TS])
            zt_ps = [ps(ph, f"zt_ps{j}", [P, 512]) for j in range(BANKS)]
            h_ps = [ps(ph, f"h_ps{j}", [P, 512]) for j in range(BANKS)]

            def tiles(j):
                return min(2, TS - 2 * j)

            def on(s):
                return not isinstance(s, int) or 0 <= s < S

            def late(s, n):
                return not isinstance(s, int) or s >= n

            with nc.Block() as block:
                @block.scalar
                def _(act):
                    def turn_out(s, u, j):
                        act.wait_ge(z_turned, s * BANKS + j + 1)
                        if late(s, 2):
                            act.wait_ge(prod_done, (s - 2) * BANKS + j + 1)
                        n = tiles(j) * D
                        nc.scalar.activation(zt[:, u, 4 * j:4 * j + 2 * tiles(j), :].rearrange("p a b -> p (a b)"),
                                             zt_ps[j][:, 0:n], ACT.Copy).then_inc(zt_copied, 1)

                    def stage(k, u):
                        if on(k):
                            if late(k, G):
                                act.wait_ge(h_done, (k - G + 1) * BANKS)
                            if late(k, 2):
                                act.wait_ge(h2_done, k - 1)
                            g = k % G
                            nc.scalar.activation(th[:, u, :, :], state[:, bass.ds(g * TS, TS), :], ACT.Tanh).then_inc(tanh_done, 1)
                        s = k - 3
                        if on(s):
                            for j in range(BANKS // 2):
                                turn_out(s, 1 - u, j)
                        s = k - 2
                        if on(s):
                            act.wait_ge(h2_done, s + 1)
                            if late(s, 2):
                                act.wait_ge(z_done, s - 1)
                            nc.scalar.activation(sg[:, u, :, :], h2[:, u, :, :], ACT.Sigmoid).then_inc(sig_done, 1)
                        s = k - 3
                        if on(s):
                            for j in range(BANKS // 2, BANKS):
                                turn_out(s, 1 - u, j)
                    pipeline(act, S, 8, 2, stage)

                @block.vector
                def _(dve):
                    v = nc.vector

                    def stage(k, u):
                        s = k - 4
                        if on(s):
                            dve.wait_ge(rstd_done, s + 1)
                            for j in range(BANKS):
                                dve.wait_ge(prod_done, s * BANKS + j + 1)
                                for a in range(tiles(j)):
                                    i = 2 * j + a
                                    last = v.scalar_tensor_tensor(
                                        state[:, bass.ds((s % G) * TS + i, 1), :].rearrange("p a d -> p (a d)"),
                                        h_ps[j][:, a * D:(a + 1) * D], zrs[:, u, i:i + 1], b_scan[:, :], ALU.mult, ALU.add)
                                last.then_inc(h_done, 1)
                        s = k - 2
                        if on(s):
                            dve.wait_ge(sig_done, s + 1)
                            if late(s, 2):
                                dve.wait_ge(z_turned, (s - 1) * BANKS)
                            v.tensor_tensor(z[:, u, :, :], h2[:, u, :, :], sg[:, u, :, :], ALU.mult).then_inc(z_done, 1)
                        s = k - 1
                        if on(s):
                            dve.wait_ge(tanh_done, s + 1)
                            if late(s, 2):
                                dve.wait_ge(sig_done, s - 1)
                            v.scalar_tensor_tensor(h2[:, 1 - u, :, :], th[:, 1 - u, :, :], RES_SCALE,
                                                   state[:, bass.ds((s % G) * TS, TS), :], ALU.mult, ALU.add).then_inc(h2_done, 1)
                        s = k - 2
                        if on(s):
                            dve.wait_ge(z_done, s + 1)
                            for i in range(TS):
                                last = v.bn_stats(zst[:, i, :], z[:, u, i, :])
                            last.then_inc(var_ch, 1)
                            dve.wait_ge(var_ch, s * 4 + 1)
                            if late(s, 2):
                                dve.wait_ge(rstd_done, s - 1)
                            v.tensor_tensor(zhalf[:, :], zst[:, :, 1], zst[:, :, 4], ALU.subtract).then_inc(var_ch, 1)
                            v.tensor_tensor(zsum[:, :], zst[:, :, 2], zst[:, :, 5], ALU.add).then_inc(var_ch, 1)
                            dve.wait_ge(var_ch, s * 4 + 3)
                            v.scalar_tensor_tensor(zhalf[:, :], zhalf[:, :], 0.25, zhalf[:, :], ALU.mult, ALU.mult).then_inc(var_ch, 1)
                            dve.wait_ge(var_ch, s * 4 + 4)
                            v.scalar_tensor_tensor(zvar[:, u, :], zsum[:, :], 1.0 / D, zhalf[:, :], ALU.mult, ALU.add).then_inc(var_done, 1)
                    pipeline(dve, S, 4, 2, stage)

                @block.gpsimd
                def _(pool):
                    def stage(s, u):
                        if on(s):
                            pool.wait_ge(var_done, s + 1)
                            if late(s, 2):
                                pool.wait_ge(h_done, (s - 1) * BANKS)
                            nc.gpsimd.tensor_tensor(zeps[:, u, :], zvar[:, u, :], eps_tile[:, 0:TS], ALU.add).then_inc(eps_added, 1)
                            pool.wait_ge(eps_added, s + 1)
                            nc.gpsimd.tensor_tensor(zrs[:, u, :], zeps[:, u, :], neg_half[:, 0:TS], ALU.pow).then_inc(rstd_done, 1)
                    pipeline(pool, S, 2, 2, stage)

                @block.tensor
                def _(pe):
                    def turn(s, u, j):
                        if late(s, 1):
                            pe.wait_ge(zt_copied, (s - 1) * BANKS + j + 1)
                        for a in range(tiles(j)):
                            for c in range(KC):
                                last = nc.tensor.transpose(zt_ps[j][:, (2 * a + c) * P:(2 * a + c + 1) * P],
                                                           z[:, u, 2 * j + a, c * P:(c + 1) * P], ident[:, :])
                        last.then_inc(z_turned, 1)

                    def multiply(s, u, j):
                        pe.wait_ge(zt_copied, s * BANKS + j + 1)
                        if late(s, 1):
                            pe.wait_ge(h_done, (s - 1) * BANKS + j + 1)
                        for a in range(tiles(j)):
                            for c in range(KC):
                                last = nc.tensor.matmul(h_ps[j][:, a * D:(a + 1) * D], zt[:, u, 4 * j + 2 * a + c, :],
                                                        w_scan[:, c, :], start=c == 0, stop=c == KC - 1)
                        last.then_inc(prod_done, 1)

                    def stage(s, u):
                        if on(s):
                            pe.wait_ge(z_done, s + 1)
                            turn(s, u, 0)
                            for j in range(1, BANKS):
                                turn(s, u, j)
                                multiply(s, u, j - 1)
                            multiply(s, u, BANKS - 1)
                    pipeline(pe, S, 2, 2, stage)

        out_made = sem("out_made")
        out_stored = sem("out_stored")
        with nc.Block() as block:
            @block.vector
            def _(dve):
                for g in range(G):
                    a = slice(g * TS, (g + 1) * TS)
                    nc.vector.tensor_tensor(state[:, a, :], state[:, a, :], resid[:, a, :], ALU.add).then_inc(out_made, 1)

            @block.sync
            def _(sp):
                for g in range(G):
                    sp.wait_ge(out_made, g + 1)
                    full = min((g + 1) * TS, T - 1)
                    sp.dma_start(out[g * TS * P:full * P, :].rearrange("(t p) d -> p t d", p=P),
                                 state[:, g * TS:full, :]).then_inc(out_stored, 16)
                sp.dma_start(out[(T - 1) * P:N, :], state[0:LAST, T - 1, :]).then_inc(out_stored, 16)
                sp.wait_ge(out_stored, 16 * (G + 1))


_INS = ["x", "src", "dst", "L0_gnn_W", "L0_gnn_b", "L0_gnn_gamma", "L0_gnn_beta",
        "L0_ffn_ln_w", "L0_ffn_ln_b", "L0_ffn_W", "L0_ffn_b"]


def kernel(**inputs):
    import numpy as _np
    import concourse.bacc as _bacc
    from concourse import mybir as _mybir
    from concourse.bass_utils import run_bass_kernel_spmd as _run

    nc = _bacc.Bacc("TRN2", target_bir_lowering=False, num_devices=1)
    arrays, args = {}, []
    for name in _INS:
        a = _np.ascontiguousarray(inputs[name])
        arrays[f"in_{name}_dram"] = a
        args.append(nc.dram_tensor(f"in_{name}_dram", a.shape, _mybir.dt.from_np(a.dtype), kind="ExternalInput").ap())
    shape = tuple(_np.shape(inputs["x"]))
    args.append(nc.dram_tensor("out_0_dram", shape, _mybir.dt.float32, kind="ExternalOutput").ap())
    build_gnn_ffn(nc, *args)
    r = _run(nc, [arrays], core_ids=[0])
    return r.results[0]["out_0_dram"]
```

```python
import concourse.bass as bass
from concourse import mybir
from contextlib import ExitStack

P = 128
F32 = mybir.dt.float32
BF16 = mybir.dt.bfloat16
F16 = mybir.dt.float16
I32 = mybir.dt.int32
ALU = mybir.AluOpType
ACT = mybir.ActivationFunctionType
AX = mybir.AxisListType

EPS = 1e-5
RES_SCALE = 0.01
N_ITERS = 30
NO_NODE = 1 << 20

TS = 7

WIN = 10
WC = 3
RING = 4
F16_TOP = 2.0 ** 14


def pipeline(eng, slots, depth, unroll, stage):
    assert depth % unroll == 0
    body = (slots - depth) // unroll
    for k in range(depth):
        stage(k, k % unroll)
    with eng.Fori(0, body) as m:
        for u in range(unroll):
            stage(m * unroll + (depth + u), u)
    for k in range(depth + body * unroll, slots + depth):
        stage(k, k % unroll)


def build_gnn_ffn(nc, x, src, dst, gnn_w, gnn_b, gnn_gamma, gnn_beta, ffn_ln_w, ffn_ln_b, ffn_w, ffn_b, out):
    N, D = x.shape
    E = src.shape[0]
    L = gnn_w.shape[0]
    KC = D // P
    T = -(-N // P)
    LAST = N - (T - 1) * P
    CB = -(-E // (P * P))
    CH = CB * P
    FULL_CB = E // (P * P)
    FULL_ROWS = (E - FULL_CB * P * P) // P
    REST = E % P
    G = T // TS
    assert G * TS == T
    WPT = -(-P // WIN)
    W_ALL = T * WPT
    WP = 91
    WG = W_ALL // WP
    assert WP * WG == W_ALL
    KEYS = WIN * T

    root = ExitStack()
    with root:
        def sem(name):
            return root.enter_context(nc.semaphore(name))

        def sb(stack, name, shape, dt=F32):
            return stack.enter_context(nc.sbuf_tensor(name, shape, dt))

        def ps(stack, name, shape, dt=F32):
            return stack.enter_context(nc.psum_tensor(name, shape, dt))

        def dram(name, shape, dt):
            return nc.dram_tensor(name, shape, dt, kind="Internal").ap()

        def row(buf, t):
            return buf[:, bass.ds(t, 1), :].rearrange("p a d -> p (a d)")

        state = sb(root, "state", [P, T, D])
        mv = sb(root, "mv", [P, T, 2])
        rstd = sb(root, "rstd", [P, T])
        neg_half = sb(root, "neg_half", [P, T])
        eps_tile = sb(root, "eps_tile", [P, TS])
        ident = sb(root, "ident", [P, P])
        flag = sb(root, "flag", [1, 1], I32)

        key_tab = dram("key_tab", [CH * P, 2], F32)
        dst_tab = dram("dst_tab", [CH, P], F32)
        src_tab = dram("src_tab", [CH, P], F32)
        most_tab = dram("chunk_most", [CB, P], F32)
        least_tab = dram("chunk_least", [CB, P], F32)
        base_tab = dram("window_base", [W_ALL], F32)
        start_tab = dram("window_start", [W_ALL], I32)
        count_tab = dram("count_tab", [T, P, T * P], F16)
        range_tab = dram("range_tab", [T, 2], F32)
        h_tab = dram("h_tab", [T * P, D], F32)

        gnn = root.enter_context(ExitStack())
        dinv = sb(gnn, "dinv", [P, T])
        degs = sb(gnn, "degs", [P, T])
        scale_up = sb(gnn, "scale_up", [P, L, T])
        scale_down = sb(gnn, "scale_down", [P, L, T])
        sigma = sb(gnn, "sigma", [P, L, 2])
        iota_row = sb(gnn, "iota_row", [P, P])
        iota_h = sb(gnn, "iota_h", [P, KEYS], F16)
        iota_part = sb(gnn, "iota_part", [P, 1])
        ident_h = sb(gnn, "ident_h", [P, P], F16)
        ones_h = sb(gnn, "ones_h", [P, 1], F16)
        half_tile = sb(gnn, "half_tile", [P, 2, L])
        ones_f = sb(gnn, "ones_f", [P, P])
        stats6 = sb(gnn, "stats6", [P, T, 6])
        w_gnn = sb(gnn, "w_gnn", [P, L, KC, D])
        rows3 = sb(gnn, "rows3", [P, L, 3, D])

        x_loaded, edges_loaded, params_loaded = sem("x_loaded"), sem("edges_loaded"), sem("params_loaded")
        pad_set, const_set = sem("pad_set"), sem("const_set")
        part_done, key_done, minmax_done, tabs_stored = sem("part_done"), sem("key_done"), sem("minmax_done"), sem("tabs_stored")
        stat_done, base_made = sem("stat_done"), sem("base_made")
        thr_loaded, most_loaded, find, idx_made, rows_got, start_stored, start_loaded = (
            sem(s) for s in ("thr_loaded", "most_loaded", "find", "idx_made", "rows_got", "start_stored", "start_loaded"))
        bound, bound_pe, bound_pool = sem("bound"), sem("bound_pe"), sem("bound_pool")
        starts = sb(gnn, "starts", [1, W_ALL], I32)

        with ExitStack() as ph:
            dst_nat = sb(ph, "dst_nat", [P, CB, P], I32)
            src_nat = sb(ph, "src_nat", [P, CB, P], I32)
            src_part = sb(ph, "src_part", [P, 2, CB, P], I32)
            dst_f = sb(ph, "dst_f", [P, CB, P])
            src_f = sb(ph, "src_f", [P, CB, P])
            tile_f = sb(ph, "tile_f", [P, CB, P])
            keys = sb(ph, "keys", [P, CB, P, 2])
            tmin = sb(ph, "tmin", [P, CB])
            tmax = sb(ph, "tmax", [P, CB])
            w_base = sb(ph, "w_base", [T, WPT])
            with nc.Block() as block:
                @block.sync
                def _(sp):
                    n_full = FULL_CB * P * P
                    n_rows = n_full + FULL_ROWS * P
                    for i, (nat, e) in enumerate(((dst_nat, dst), (src_nat, src))):
                        sp.dma_start(nat[:, 0:FULL_CB, :],
                                     e[0:n_full].rearrange("(b p e) -> p b e", p=P, e=P)).then_inc(edges_loaded, 16)
                        sp.wait_ge(pad_set, i + 1)
                        sp.dma_start(nat[0:FULL_ROWS, FULL_CB, :],
                                     e[n_full:n_rows].rearrange("(p e) -> p e", e=P)).then_inc(edges_loaded, 16)
                        sp.dma_start(nat[FULL_ROWS:FULL_ROWS + 1, FULL_CB, 0:REST],
                                     e[n_rows:E].rearrange("(p e) -> p e", p=1)).then_inc(edges_loaded, 16)
                    sp.dma_start(state[:, 0:T - 1, :],
                                 x[0:(T - 1) * P, :].rearrange("(t p) d -> p t d", p=P)).then_inc(x_loaded, 16)
                    sp.wait_ge(pad_set, 3)
                    sp.dma_start(state[0:LAST, T - 1, :], x[(T - 1) * P:N, :]).then_inc(x_loaded, 16)
                    sp.wait_ge(base_made, 1)
                    sp.dma_start(base_tab.rearrange("(t j) -> t j", t=T), w_base[:, :]).then_inc(tabs_stored, 16)
                    sp.wait_ge(part_done, 3)
                    for b in range(CB):
                        sp.dma_start(dst_tab[b * P:(b + 1) * P, :], dst_f[:, b, :]).then_inc(tabs_stored, 16)
                        sp.dma_start(src_tab[b * P:(b + 1) * P, :], src_f[:, b, :]).then_inc(tabs_stored, 16)
                    sp.wait_ge(minmax_done, 2)
                    with nc.allow_non_contiguous_dma(reason="two small tables"):
                        sp.dma_start(least_tab.rearrange("b p -> p b"), tmin[:, :]).then_inc(tabs_stored, 16)
                        sp.dma_start(most_tab.rearrange("b p -> p b"), tmax[:, :]).then_inc(tabs_stored, 16)
                    sp.wait_ge(key_done, 2)
                    sp.dma_start(key_tab.rearrange("(b p e) c -> p b (e c)", p=P, e=P),
                                 keys[:, :, :, :].rearrange("p b e c -> p b (e c)")).then_inc(tabs_stored, 16)
                    sp.wait_ge(tabs_stored, 16 * (2 * CB + 4))

                @block.scalar
                def _(act):
                    for i in range(L):
                        act.dma_start(w_gnn[:, i, :, :],
                                      gnn_w[i, :, :].rearrange("(k p) d -> p k d", p=P)).then_inc(params_loaded, 16)
                        for j, v in enumerate((gnn_b, gnn_gamma, gnn_beta)):
                            act.dma_start(rows3[:, i, j, :],
                                          v[i:i + 1, :].partition_broadcast(P)).then_inc(params_loaded, 16)
                    act.wait_ge(params_loaded, 16 * 4 * L)

                @block.gpsimd
                def _(pool):
                    g = nc.gpsimd
                    g.iota(w_base[:, :], [[WIN, WPT]], base=0, channel_multiplier=P,
                           allow_small_or_imprecise_dtypes=True).then_inc(base_made, 1)
                    g.iota(iota_row[:, :], [[1, P]], base=0, channel_multiplier=0, allow_small_or_imprecise_dtypes=True)
                    g.iota(iota_h[:, :], [[1, KEYS]], base=0, channel_multiplier=0, allow_small_or_imprecise_dtypes=True)
                    g.iota(iota_part[:, :], [[0, 1]], base=0, channel_multiplier=1, allow_small_or_imprecise_dtypes=True)
                    g.memset(neg_half[:, :], -0.5)
                    g.memset(eps_tile[:, :], EPS)
                    g.memset(half_tile[:, :, :], 0.5)
                    g.memset(ones_h[:, :], 1.0)
                    g.memset(ones_f[:, :], 1.0)
                    g.memset(ident[:, :], 0.0).then_inc(const_set, 1)
                    pool.wait_ge(const_set, 1)
                    g.affine_select(out=ident[:, :], in_=ident[:, :], compare_op=ALU.not_equal, fill=1.0,
                                    base=0, pattern=[[-1, P]], channel_multiplier=1).then_inc(const_set, 1)
                    pool.wait_ge(const_set, 2)
                    g.tensor_copy(ident_h[:, :], ident[:, :])

                @block.vector
                def _(dve):
                    v = nc.vector
                    v.memset(dst_nat[:, FULL_CB, :], NO_NODE).then_inc(pad_set, 1)
                    v.memset(src_nat[:, FULL_CB, :], 0).then_inc(pad_set, 1)
                    v.memset(state[:, T - 1, :], 0.0).then_inc(pad_set, 1)
                    dve.wait_ge(edges_loaded, 96)
                    v.tensor_copy(dst_f[:, :, :], dst_nat[:, :, :]).then_inc(part_done, 1)
                    v.tensor_copy(src_f[:, :, :], src_nat[:, :, :]).then_inc(part_done, 1)
                    v.tensor_scalar(src_part[:, 1, :, :], src_nat[:, :, :], P - 1, None, ALU.bitwise_and)
                    v.tensor_scalar(src_part[:, 0, :, :], src_nat[:, :, :], P.bit_length() - 1, None,
                                    ALU.arith_shift_right).then_inc(part_done, 1)
                    dve.wait_ge(part_done, 3)
                    v.tensor_reduce(tmin[:, :], dst_f[:, :, :], AX.X, ALU.min).then_inc(minmax_done, 1)
                    v.tensor_reduce(tmax[:, :], dst_f[:, :, :], AX.X, ALU.max).then_inc(minmax_done, 1)
                    v.tensor_copy(keys[:, :, :, 1], src_part[:, 1, :, :]).then_inc(key_done, 1)
                    v.tensor_copy(tile_f[:, :, :], src_part[:, 0, :, :]).then_inc(part_done, 1)
                    dve.wait_ge(part_done, 4)
                    v.scalar_tensor_tensor(keys[:, :, :, 0], dst_f[:, :, :], float(T), tile_f[:, :, :],
                                           ALU.mult, ALU.add).then_inc(key_done, 1)
                    dve.wait_ge(x_loaded, 32)
                    for t in range(T):
                        v.bn_stats(stats6[:, t, :], state[:, t, :])

        with ExitStack() as ph:
            most = sb(ph, "most", [P, CH])
            junk = sb(ph, "junk", [P, CH])
            thr = sb(ph, "thr", [WP, WG])
            whole = sb(ph, "whole", [WP, WG])
            rest = sb(ph, "rest", [WP, WG])
            start_f = sb(ph, "start_f", [WP, WG])
            idx = sb(ph, "idx", [WP, WG], I32)
            start_i = sb(ph, "start_i", [WP, WG], I32)
            got = sb(ph, "got", [WP, WG, P])
            wsum = sb(ph, "wsum", [P, L])
            bsum = sb(ph, "bsum", [P, L])
            gmax = sb(ph, "gmax", [P, L])
            sq = sb(ph, "sq", [P, KC * D])
            norm = sb(ph, "norm", [P, 2, L])
            xnorm = sb(ph, "xnorm", [P, L])
            wsum_ps = ps(ph, "wsum_ps", [P, L])
            with nc.Block() as block:
                @block.sync
                def _(sp):
                    sp.dma_start(most[0:WP, :], most_tab.rearrange("b p -> (b p)").partition_broadcast(WP)).then_inc(most_loaded, 16)
                    sp.dma_start(thr[:, :], base_tab.rearrange("(p g) -> p g", g=WG)).then_inc(thr_loaded, 16)
                    sp.wait_ge(find, 2 * WG + 3)
                    sp.dma_start(start_tab.rearrange("(p g) -> p g", g=WG), start_i[:, :]).then_inc(start_stored, 16)
                    sp.wait_ge(start_stored, 16)
                    sp.dma_start(starts[:, :], start_tab.rearrange("(a w) -> a w", a=1)).then_inc(start_loaded, 16)
                    sp.wait_ge(start_loaded, 16)

                @block.gpsimd
                def _(pool):
                    pool.wait_ge(idx_made, 1)
                    for g in range(WG):
                        nc.gpsimd.indirect_dma_start(got[:, g, :], None, dst_tab[:, :],
                                                     bass.IndirectOffsetOnAxis(idx[:, g:g + 1], 0)).then_inc(rows_got, 16)
                    pool.wait_ge(bound, 3 * L + 2)
                    nc.gpsimd.tensor_tensor(norm[:, :, :], norm[:, :, :], half_tile[:, :, :], ALU.pow).then_inc(bound_pool, 1)

                @block.tensor
                def _(pe):
                    pe.wait_ge(bound, L)
                    nc.tensor.matmul(wsum_ps[:, :], ones_f[:, :], wsum[:, :], start=True, stop=True).then_inc(bound_pe, 1)

                @block.vector
                def _(dve):
                    v = nc.vector
                    dve.wait_ge(most_loaded, 16)
                    dve.wait_ge(thr_loaded, 16)
                    for g in range(WG):
                        if g >= 1:
                            dve.wait_ge(find, g)
                        v.tensor_scalar(junk[0:WP, :], most[0:WP, :], thr[:, g:g + 1], None, ALU.is_lt, ALU.add,
                                        accum_out=whole[:, g:g + 1]).then_inc(find, 1)
                    dve.wait_ge(find, WG)
                    v.tensor_copy(idx[:, :], whole[:, :]).then_inc(idx_made, 1)
                    for i in range(L):
                        if i >= 1:
                            dve.wait_ge(bound, i)
                        v.tensor_tensor_reduce(out=sq[:, :], in0=w_gnn[:, i, :, :].rearrange("p k d -> p (k d)"),
                                               in1=w_gnn[:, i, :, :].rearrange("p k d -> p (k d)"), scale=1.0, scalar=0.0,
                                               op0=ALU.mult, op1=ALU.add, accum_out=wsum[:, i:i + 1]).then_inc(bound, 1)
                    for i in range(L):
                        dve.wait_ge(bound, L + 2 * i)
                        v.tensor_tensor_reduce(out=sq[:, 0:D], in0=rows3[:, i, 2, :], in1=rows3[:, i, 2, :], scale=1.0,
                                               scalar=0.0, op0=ALU.mult, op1=ALU.add,
                                               accum_out=bsum[:, i:i + 1]).then_inc(bound, 1)
                        v.tensor_reduce(gmax[:, i:i + 1], rows3[:, i, 1, :], AX.X, ALU.max,
                                        apply_absolute_value=True).then_inc(bound, 1)
                    dve.wait_ge(bound, 3 * L)
                    v.tensor_copy(norm[:, 1, :], bsum[:, :]).then_inc(bound, 1)
                    dve.wait_ge(bound_pe, 1)
                    v.tensor_copy(norm[:, 0, :], wsum_ps[:, :]).then_inc(bound, 1)
                    dve.wait_ge(bound_pool, 1)
                    n = [3 * L + 2]

                    def link(ins):
                        n[0] += 1
                        ins.then_inc(bound, 1)
                        dve.wait_ge(bound, n[0])
                    link(v.memset(xnorm[:, 0:1], float(D) ** 0.5))
                    link(v.scalar_tensor_tensor(xnorm[:, 1:L], gmax[:, 0:L - 1], float(D) ** 0.5, norm[:, 1, 0:L - 1],
                                                ALU.mult, ALU.add))
                    link(v.tensor_tensor(xnorm[:, :], xnorm[:, :], norm[:, 0, :], ALU.mult))
                    link(v.tensor_scalar(xnorm[:, :], xnorm[:, :], 1e-30, 1.0 / F16_TOP, ALU.max, ALU.mult))
                    v.tensor_copy(sigma[:, :, 1], xnorm[:, :])
                    link(v.reciprocal(sigma[:, :, 0], xnorm[:, :]))
                    for g in range(WG):
                        dve.wait_ge(rows_got, 16 * WG)
                        dve.wait_ge(find, WG + g)
                        v.tensor_scalar(junk[0:WP, 0:P], got[:, g, :], thr[:, g:g + 1], None, ALU.is_lt, ALU.add,
                                        accum_out=rest[:, g:g + 1]).then_inc(find, 1)
                    dve.wait_ge(find, 2 * WG)
                    v.scalar_tensor_tensor(start_f[:, :], whole[:, :], float(P), rest[:, :], ALU.mult, ALU.add).then_inc(find, 1)
                    dve.wait_ge(find, 2 * WG + 1)
                    v.tensor_copy(start_i[:, :], start_f[:, :]).then_inc(find, 1)
                    dve.wait_ge(find, 2 * WG + 2)
                    dve.sem_inc(find, 1)

        ev_loaded = [sem(f"ev_loaded{u}") for u in range(2)]
        strip_stored = [sem(f"strip_stored{u}") for u in range(2)]
        hots_made, win_done, win_out, deg_made, deg_out, base_ch = (
            sem(s) for s in ("hots_made", "win_done", "win_out", "deg_made", "deg_out", "base_ch"))
        with ExitStack() as ph:
            ev = sb(ph, "ev", [P, 2, WPT, WC, 2])
            key_rel = sb(ph, "key_rel", [P, 2, WPT, WC])
            first_key = sb(ph, "first_key", [P, WPT])
            hot_key = sb(ph, "hot_key", [P, WPT, WC, KEYS], F16)
            hot_src = sb(ph, "hot_src", [P, WPT, WC, P], F16)
            strip = sb(ph, "strip", [P, 2, T, P], F16)
            win_ps = [ps(ph, f"win_ps{i}", [P, 512]) for i in range(2)]
            deg_ps = [ps(ph, f"deg_ps{i}", [P, 512]) for i in range(2)]

            def width(j):
                return min(WIN, P - WIN * j)

            with nc.Block() as block:
                def is_tile(t):
                    return not isinstance(t, int) or 0 <= t < T

                def late(t, n):
                    return not isinstance(t, int) or t >= n

                @block.sync
                def _(sp):
                    def stage(k, u):
                        if is_tile(k):
                            if late(k, 2):
                                sp.wait_ge(hots_made, (k - 1) * WPT)
                            for j in range(WPT):
                                e0 = sp.value_load(starts[0:1, bass.ds(k * WPT + j, 1)], min_val=0, max_val=E)
                                sp.dma_start(ev[:, u, j, :, :].rearrange("p c k -> p (c k)"),
                                             key_tab[bass.ds(e0, WC * P), :].rearrange("(p c) k -> p (c k)", c=WC))\
                                  .then_inc(ev_loaded[u], 16)
                    pipeline(sp, T, 2, 2, stage)
                    sp.wait_ge(strip_stored[0], 16 * ((T + 1) // 2))
                    sp.wait_ge(strip_stored[1], 16 * (T // 2))

                @block.vector
                def _(dve):
                    v = nc.vector
                    v.tensor_scalar(first_key[:, :], iota_row[:, 0:WPT], float(WIN * T), None, ALU.mult).then_inc(base_ch, 1)

                    def stage(k, u):
                        if not is_tile(k):
                            return
                        dve.wait_ge(ev_loaded[u], (k - u) * (8 * WPT) + 16 * WPT)
                        dve.wait_ge(base_ch, 2 * k + 1)
                        v.tensor_tensor(key_rel[:, u, :, :], ev[:, u, :, :, 0],
                                        first_key[:, :].unsqueeze(2).to_broadcast([P, WPT, WC]), ALU.subtract).then_inc(base_ch, 1)
                        dve.wait_ge(base_ch, 2 * k + 2)
                        v.tensor_scalar(first_key[:, :], first_key[:, :], float(P * T), None, ALU.add).then_inc(base_ch, 1)
                        for j in range(WPT):
                            if late(k, 1):
                                dve.wait_ge(win_done, (k - 1) * WPT + j + 1)
                            for c in range(WC):
                                v.tensor_scalar(hot_src[:, j, c, :], iota_h[:, 0:P], ev[:, u, j, c, 1:2], None, ALU.is_equal)
                                last = v.tensor_scalar(hot_key[:, j, c, :], iota_h[:, :], key_rel[:, u, j, c:c + 1], None,
                                                       ALU.is_equal)
                            last.then_inc(hots_made, 1)
                    pipeline(dve, T, 2, 2, stage)

                @block.tensor
                def _(pe):
                    def degrees(t, u):
                        pe.wait_ge(win_out, (t + 1) * WPT)
                        if late(t, 2):
                            pe.wait_ge(deg_out, t - 1)
                        for s in range(T):
                            last = nc.tensor.matmul(deg_ps[u][:, 0:1], strip[:, u, s, :], ones_h[:, :], start=s == 0, stop=s == T - 1)
                        last.then_inc(deg_made, 1)

                    def stage(k, u):
                        if is_tile(k):
                            for j in range(WPT):
                                pe.wait_ge(hots_made, k * WPT + j + 1)
                                b = (u * WPT + j) % 2
                                if j >= 2 or late(k, 1):
                                    pe.wait_ge(win_out, k * WPT + j - 1)
                                for c in range(WC):
                                    last = nc.tensor.matmul(win_ps[b][:, 0:KEYS], hot_src[:, j, c, :], hot_key[:, j, c, :],
                                                            start=c == 0, stop=c == WC - 1)
                                last.then_inc(win_done, 1)
                                if j == 4 and is_tile(k - 1) and late(k, 1):
                                    degrees(k - 1, 1 - u)
                        elif k == T:
                            degrees(k - 1, 1 - u)
                    pipeline(pe, T, 4, 2, stage)

                @block.scalar
                def _(act):
                    def deg_copy(t, u):
                        act.wait_ge(deg_made, t + 1)
                        nc.scalar.activation(degs[:, bass.ds(t, 1)], deg_ps[u][:, 0:1], ACT.Copy).then_inc(deg_out, 1)

                    def stage(k, u):
                        if is_tile(k):
                            for j in range(WPT):
                                if j == 0 and late(k, 2):
                                    act.wait_ge(deg_made, k - 1)
                                    act.wait_ge(strip_stored[u], (k - u) * 8)
                                act.wait_ge(win_done, k * WPT + j + 1)
                                b = (u * WPT + j) % 2
                                w = width(j)
                                nc.scalar.activation(
                                    strip[:, u, :, WIN * j:WIN * j + w].rearrange("p s d -> p d s"),
                                    win_ps[b][:, 0:w * T].rearrange("p (d s) -> p d s", d=w), ACT.Copy).then_inc(win_out, 1)
                                if j == 8 and is_tile(k - 1) and late(k, 1):
                                    deg_copy(k - 1, 1 - u)
                            act.wait_ge(win_out, (k + 1) * WPT)
                            act.dma_start(count_tab[bass.ds(k, 1), :, :].rearrange("a p m -> p (a m)"),
                                          strip[:, u, :, :].rearrange("p s d -> p (s d)")).then_inc(strip_stored[u], 16)
                        elif k == T:
                            deg_copy(k - 1, 1 - u)
                    pipeline(act, T, 2, 2, stage)

        total_made, total_done, flag_made, flag_checked = (sem(s) for s in ("total_made", "total_done", "flag_made", "flag_checked"))
        with ExitStack() as ph:
            part_sum = sb(ph, "part_sum", [P, 1])
            total_ps = ps(ph, "total_ps", [P, 1])
            with nc.Block() as block:
                @block.vector
                def _(dve):
                    nc.vector.tensor_reduce(part_sum[:, :], degs[:, :], AX.X, ALU.add).then_inc(total_made, 1)
                    dve.wait_ge(total_done, 1)
                    nc.vector.tensor_scalar(flag[:, :], total_ps[0:1, :], float(E), None, ALU.is_equal).then_inc(flag_made, 1)

                @block.tensor
                def _(pe):
                    pe.wait_ge(total_made, 1)
                    nc.tensor.matmul(total_ps[:, :], ones_f[:, :], part_sum[:, :], start=True, stop=True).then_inc(total_done, 1)

        def counted(eng):
            return eng.value_load(flag[0:1, 0:1], min_val=0, max_val=1)

        h_stack = gnn.enter_context(ExitStack())
        h_split = sb(h_stack, "h_split", [P, T, 2 * D], F16)
        strips = sb(h_stack, "strips", [P, RING, T * P], F16)
        half_strip = T * P // 2
        assert CH <= half_strip
        dst_col = strips[:, 0, :].bitcast(F32)[:, 0:CH]
        src_col = strips[:, 1, :].bitcast(I32)[:, 0:CH]
        tab = sb(h_stack, "tab", [1, T, 4], I32)

        U = 8
        g_loaded, g_turned, g_out, split_done, onehots_ready, onehots_used, deg_done = (
            sem(s) for s in ("g_loaded", "g_turned", "g_out", "split_done", "onehots_ready", "onehots_used", "deg_done"))
        rows_loaded, rng, tab_stored, tab_loaded, cnt_ready, kdown_set = (
            sem(s) for s in ("rows_loaded", "rng", "tab_stored", "tab_loaded", "cnt_ready", "kdown_set"))
        with ExitStack() as ph:
            nat = sb(ph, "nat", [P, 2, P])
            part_i = strips[:, 2, :].bitcast(I32)[:, 0:CH]
            dst_i = strips[:, 3, :].bitcast(I32)[:, 0:CH]
            row_f = h_split[:, :, :].rearrange("p t d -> p (t d)")[:, 0:2 * CH].bitcast(F32)
            tile_f = h_split[:, :, :].rearrange("p t d -> p (t d)")[:, 2 * CH:4 * CH].bitcast(F32)
            zero_h = sb(ph, "zero_h", [P, P], F16)
            hot_row = sb(ph, "hot_row", [P, U, P], F16)
            hot_tile = sb(ph, "hot_tile", [P, U, T], F16)
            tr = [ps(ph, f"tr{i}", [P, 512]) for i in range(2)]
            deg_ps = ps(ph, "gdeg_ps", [P, T])
            with nc.Block() as block:
                @block.sync
                def _(sp):
                    with sp.If(counted(sp) == 0):
                        for b in range(CB):
                            if b >= 1:
                                sp.wait_ge(g_turned, 2 * b)
                            sp.dma_start(nat[:, 0, :], dst_tab[b * P:(b + 1) * P, :]).then_inc(g_loaded, 16)
                            sp.dma_start(nat[:, 1, :], src_tab[b * P:(b + 1) * P, :]).then_inc(g_loaded, 16)

                @block.tensor
                def _(pe):
                    with pe.If(counted(pe) == 0):
                        for b in range(CB):
                            pe.wait_ge(g_loaded, 32 * (b + 1))
                            if b >= 1:
                                pe.wait_ge(g_out, 2 * b)
                            for i in range(2):
                                nc.tensor.transpose(tr[i][:, 0:P], nat[:, i, :], ident[:, :]).then_inc(g_turned, 1)
                        pe.wait_ge(split_done, 1)
                        nc.tensor.matmul(deg_ps[:, :], zero_h[:, :], zero_h[:, 0:T], start=True, stop=False)
                        with pe.Fori(0, CH // U) as it:
                            for u in range(U):
                                pe.wait_ge(onehots_ready, it * U + u + 1)
                                nc.tensor.matmul(deg_ps[:, :], hot_row[:, u, :], hot_tile[:, u, :], start=False,
                                                 stop=False).then_inc(onehots_used, 1)
                        nc.tensor.matmul(deg_ps[:, :], zero_h[:, :], zero_h[:, 0:T], start=False, stop=True).then_inc(deg_done, 1)

                @block.vector
                def _(dve):
                    v = nc.vector
                    with dve.If(counted(dve) == 0):
                        v.memset(zero_h[:, :], 0.0).then_inc(split_done, 1)
                        for b in range(CB):
                            dve.wait_ge(g_turned, 2 * b + 2)
                            v.tensor_copy(dst_col[:, b * P:(b + 1) * P], tr[0][:, 0:P]).then_inc(g_out, 1)
                            v.tensor_copy(src_col[:, b * P:(b + 1) * P], tr[1][:, 0:P]).then_inc(g_out, 1)
                        dve.wait_ge(g_out, 2 * CB)
                        v.tensor_copy(dst_i, dst_col).then_inc(split_done, 1)
                        dve.wait_ge(split_done, 2)
                        v.tensor_scalar(part_i, dst_i, P - 1, None, ALU.bitwise_and).then_inc(split_done, 1)
                        dve.wait_ge(split_done, 3)
                        v.tensor_copy(row_f, part_i).then_inc(split_done, 1)
                        dve.wait_ge(split_done, 4)
                        v.tensor_scalar(part_i, dst_i, P.bit_length() - 1, None, ALU.arith_shift_right).then_inc(split_done, 1)
                        dve.wait_ge(split_done, 5)
                        v.tensor_copy(tile_f, part_i).then_inc(split_done, 1)
                        dve.wait_ge(split_done, 6)

                        def chunks(it, first):
                            for u in range(U):
                                k = it * U + u
                                if not first:
                                    dve.wait_ge(onehots_used, (it - 1) * U + u + 1)
                                v.tensor_scalar(hot_row[:, u, :], iota_h[:, 0:P], row_f[:, bass.ds(k, 1)], None, ALU.is_equal)
                                v.tensor_scalar(hot_tile[:, u, :], iota_h[:, 0:T], tile_f[:, bass.ds(k, 1)], None,
                                                ALU.is_equal).then_inc(onehots_ready, 1)
                        chunks(0, True)
                        with dve.Fori(1, CH // U) as it:
                            chunks(it, False)
                        dve.wait_ge(deg_done, 1)
                        v.tensor_copy(degs[:, :], deg_ps[:, :]).then_inc(split_done, 1)

        with ExitStack() as ph:
            least = sb(ph, "least", [P, CH])
            most = sb(ph, "most_b", [P, CH])
            kup = strips[:, 2, :].bitcast(F32)[:, 0:CH]
            kdown = strips[:, 3, :].bitcast(F32)[:, 0:CH]
            thr = sb(ph, "thr_t", [P, 2])
            ends = sb(ph, "ends", [P, 4])
            pair = sb(ph, "pair", [P, 2])
            line = sb(ph, "line", [1, T, 2])
            cum = sb(ph, "cum", [1, T])
            zline = sb(ph, "zline", [1, T])
            tab_f = sb(ph, "tab_f", [1, T, 4])
            with nc.Block() as block:
                @block.sync
                def _(sp):
                    with sp.If(counted(sp) == 0):
                        sp.dma_start(least[:, :], least_tab.rearrange("b p -> (b p)").partition_broadcast(P)).then_inc(rows_loaded, 16)
                        sp.dma_start(most[:, :], most_tab.rearrange("b p -> (b p)").partition_broadcast(P)).then_inc(rows_loaded, 16)
                        sp.wait_ge(cnt_ready, 1)
                        sp.dma_start(range_tab[:, :], pair[0:T, :]).then_inc(tab_stored, 16)
                        sp.wait_ge(tab_stored, 16)
                        sp.dma_start(line[:, :, :], range_tab.rearrange("(a t) c -> a t c", a=1)).then_inc(tab_loaded, 16)
                        sp.wait_ge(tab_loaded, 16)

                @block.gpsimd
                def _(pool):
                    with pool.If(counted(pool) == 0):
                        nc.gpsimd.iota(kup, [[1, CH]], base=1, channel_multiplier=0,
                                       allow_small_or_imprecise_dtypes=True)
                        nc.gpsimd.iota(kdown, [[-1, CH]], base=CH, channel_multiplier=0,
                                       allow_small_or_imprecise_dtypes=True).then_inc(kdown_set, 1)

                @block.vector
                def _(dve):
                    n = [0]

                    def link(ins):
                        n[0] += 1
                        ins.then_inc(rng, 1)
                        dve.wait_ge(rng, n[0])
                    v = nc.vector
                    with dve.If(counted(dve) == 0):
                        v.tensor_scalar(thr[:, 0:1], iota_part[:, :], float(P), None, ALU.mult)
                        link(v.tensor_scalar(thr[:, 1:2], iota_part[:, :], float(P), float(P - 1), ALU.mult, ALU.add))
                        dve.wait_ge(rows_loaded, 32)
                        dve.wait_ge(kdown_set, 1)
                        link(v.scalar_tensor_tensor(most[:, :], most[:, :], thr[:, 0:1], kdown, ALU.is_ge, ALU.mult))
                        link(v.scalar_tensor_tensor(least[:, :], least[:, :], thr[:, 1:2], kup, ALU.is_le, ALU.mult))
                        link(v.tensor_reduce(ends[:, 0:1], most[:, :], AX.X, ALU.max))
                        link(v.tensor_reduce(ends[:, 1:2], least[:, :], AX.X, ALU.max))
                        link(v.tensor_scalar(pair[:, 0:1], ends[:, 0:1], -1.0, float(CH), ALU.mult, ALU.add))
                        link(v.tensor_tensor(ends[:, 2:3], ends[:, 1:2], pair[:, 0:1], ALU.subtract))
                        v.tensor_scalar(pair[:, 1:2], ends[:, 2:3], 1.0, None, ALU.max).then_inc(cnt_ready, 1)
                        link(v.memset(zline[:, :], 0.0))
                        dve.wait_ge(tab_loaded, 16)
                        link(v.tensor_tensor_scan(cum[:, :], line[:, :, 1], zline[:, :], 0.0, ALU.add, ALU.add))
                        link(v.tensor_tensor(tab_f[:, :, 0], cum[:, :], line[:, :, 1], ALU.subtract))
                        v.tensor_copy(tab_f[:, :, 1], line[:, :, 1])
                        v.tensor_copy(tab_f[:, :, 3], line[:, :, 1])
                        link(v.tensor_copy(tab_f[:, :, 2], line[:, :, 0]))
                        link(v.tensor_copy(tab[:, :, :], tab_f[:, :, :]))

        deg1_made, dinv_made = sem("deg1_made"), sem("dinv_made")
        with nc.Block() as block:
            @block.vector
            def _(dve):
                nc.vector.tensor_scalar(degs[:, :], degs[:, :], 1.0, None, ALU.add).then_inc(deg1_made, 1)
                dve.wait_ge(dinv_made, 1)
                for i in range(L):
                    nc.vector.tensor_scalar(scale_up[:, i, :], dinv[:, :], sigma[:, i, 0:1], None, ALU.mult)
                    nc.vector.tensor_scalar(scale_down[:, i, :], dinv[:, :], sigma[:, i, 1:2], None, ALU.mult)

            @block.gpsimd
            def _(pool):
                pool.wait_ge(deg1_made, 1)
                nc.gpsimd.tensor_tensor(dinv[:, :], degs[:, :], neg_half[:, :], ALU.pow).then_inc(dinv_made, 1)

        stat_steps, rstd_ready = sem("stat_steps"), sem("rstd_ready")

        def rstd_of_rows(name, turn):
            small, base = stat_steps, 7 * turn
            with ExitStack() as ph:
                half = sb(ph, f"{name}_half", [P, T])
                with nc.Block() as block:
                    @block.vector
                    def _(dve):
                        v = nc.vector
                        v.tensor_tensor(mv[:, :, 0], stats6[:, :, 1], stats6[:, :, 4], ALU.add).then_inc(small, 1)
                        v.tensor_tensor(half[:, :], stats6[:, :, 1], stats6[:, :, 4], ALU.subtract).then_inc(small, 1)
                        v.tensor_tensor(mv[:, :, 1], stats6[:, :, 2], stats6[:, :, 5], ALU.add).then_inc(small, 1)
                        dve.wait_ge(small, base + 3)
                        v.tensor_scalar(mv[:, :, 0], mv[:, :, 0], 0.5, None, ALU.mult).then_inc(small, 1)
                        v.scalar_tensor_tensor(half[:, :], half[:, :], 0.25, half[:, :], ALU.mult, ALU.mult).then_inc(small, 1)
                        v.tensor_scalar(mv[:, :, 1], mv[:, :, 1], 1.0 / D, EPS, ALU.mult, ALU.add).then_inc(small, 1)
                        dve.wait_ge(small, base + 6)
                        v.tensor_tensor(mv[:, :, 1], mv[:, :, 1], half[:, :], ALU.add).then_inc(small, 1)

                    @block.gpsimd
                    def _(pool):
                        pool.wait_ge(small, base + 7)
                        nc.gpsimd.tensor_tensor(rstd[:, :], mv[:, :, 1], neg_half[:, :], ALU.pow).then_inc(rstd_ready, 1)

        def layer_input(dve, i, t, xr, dch, base):
            v = nc.vector
            tt = bass.ds(t, 1)
            v.tensor_scalar(xr, row(state, t), mv[:, tt, 0:1].rearrange("p a c -> p (a c)"), rstd[:, tt],
                            ALU.subtract, ALU.mult).then_inc(dch, 1)
            if i > 0:
                dve.wait_ge(dch, base + 1)
                v.tensor_tensor(xr, xr, rows3[:, i - 1, 1, :], ALU.mult).then_inc(dch, 1)
                dve.wait_ge(dch, base + 2)
                v.tensor_tensor(xr, xr, rows3[:, i - 1, 2, :], ALU.add).then_inc(dch, 1)
                dve.wait_ge(dch, base + 3)
                v.tensor_scalar(xr, xr, 0.0, None, ALU.max).then_inc(dch, 1)

        x_made, x_turned, xt_copied, prod, hi_made, lo_made, dch = (
            sem(s) for s in ("x_made", "x_turned", "xt_copied", "prod", "hi_made", "lo_made", "input_steps"))

        def layer_product(i):
            nm = f"l{i}p"
            per = 1 if i == 0 else 4
            b = i * T
            bd = 0 if i == 0 else T + (i - 1) * T * per
            with ExitStack() as ph:
                xr = sb(ph, f"{nm}_xr", [P, 2, D])
                xt = sb(ph, f"{nm}_xt", [P, 2, KC, P])
                xt_ps = ps(ph, f"{nm}_xt_ps", [P, 2, 512])
                h_ps = ps(ph, f"{nm}_h_ps", [P, 2, 512])
                with nc.Block() as block:
                    def is_tile(t):
                        return not isinstance(t, int) or 0 <= t < T

                    def late(t, n):
                        return not isinstance(t, int) or t >= n

                    @block.vector
                    def _(dve):
                        def stage(k, u):
                            if is_tile(k):
                                if late(k, 2):
                                    dve.wait_ge(x_turned, b + k - 1)
                                layer_input(dve, i, k, xr[:, u, :], dch, bd + k * per)
                                dve.wait_ge(dch, bd + (k + 1) * per)
                                dve.sem_inc(x_made, 1)
                            t = k - 2
                            if is_tile(t) and late(k, 2):
                                dve.wait_ge(hi_made, b + t + 1)
                                nc.vector.scalar_tensor_tensor(row(h_split, t)[:, D:2 * D], h_ps[:, u, 0:D],
                                                               scale_up[:, i, bass.ds(t, 1)], row(h_split, t)[:, 0:D],
                                                               ALU.mult, ALU.subtract).then_inc(lo_made, 1)
                        pipeline(dve, T, 2, 2, stage)

                    @block.tensor
                    def _(pe):
                        def stage(k, u):
                            if is_tile(k):
                                pe.wait_ge(x_made, b + k + 1)
                                if late(k, 2):
                                    pe.wait_ge(xt_copied, b + k - 1)
                                for c in range(KC):
                                    last = nc.tensor.transpose(xt_ps[:, u, c * P:(c + 1) * P],
                                                               xr[:, u, c * P:(c + 1) * P], ident[:, :])
                                last.then_inc(x_turned, 1)
                            t = k - 1
                            if is_tile(t):
                                pe.wait_ge(xt_copied, b + t + 1)
                                if late(k, 4):
                                    pe.wait_ge(lo_made, b + t - 1)
                                for c in range(KC):
                                    last = nc.tensor.matmul(h_ps[:, 1 - u, 0:D], xt[:, 1 - u, c, :], w_gnn[:, i, c, :],
                                                            start=c == 0, stop=c == KC - 1)
                                last.then_inc(prod, 1)
                        pipeline(pe, T, 4, 2, stage)

                    @block.scalar
                    def _(act):
                        def stage(k, u):
                            if is_tile(k):
                                act.wait_ge(x_turned, b + k + 1)
                                if late(k, 2):
                                    act.wait_ge(prod, b + k - 1)
                                nc.scalar.activation(xt[:, u, :, :].rearrange("p c n -> p (c n)"), xt_ps[:, u, 0:D],
                                                     ACT.Copy).then_inc(xt_copied, 1)
                            t = k - 1
                            if is_tile(t):
                                act.wait_ge(prod, b + t + 1)
                                nc.scalar.activation(row(h_split, t)[:, 0:D], h_ps[:, 1 - u, 0:D], ACT.Copy,
                                                     scale=scale_up[:, i, bass.ds(t, 1)]).then_inc(hi_made, 1)
                        pipeline(act, T, 2, 2, stage)

        def layer_sum(i):
            nm = f"l{i}s"
            c_loaded = [sem(f"{nm}_c_loaded{r}") for r in range(RING)]
            strip_done, low_out, both, biased, seen = (sem(f"{nm}_{s}") for s in ("strip_done", "low_out", "both", "biased", "seen"))
            whole_made, h_stored, idx_ready, idx_seen, rows_ready, hot_ready, summed, free, iota_set, g_biased = (
                sem(f"{nm}_{s}") for s in ("whole", "h_stored", "idx", "idx_seen", "rows", "hot", "summed", "free", "iota", "g_biased"))
            with ExitStack() as ph:
                low = sb(ph, f"{nm}_low", [P, 2, D])
                total = sb(ph, f"{nm}_total", [P, 2, D])
                idx = sb(ph, f"{nm}_idx", [P, 1], I32)
                rows = sb(ph, f"{nm}_rows", [P, D])
                hot = sb(ph, f"{nm}_hot", [P, P])
                tile_iota = sb(ph, f"{nm}_iota_t", [P, P])
                acc = [ps(ph, f"{nm}_acc{r}", [P, 512]) for r in range(RING)]
                sum_ps = ps(ph, f"{nm}_ps", [P, D])

                def is_tile(t):
                    return not isinstance(t, int) or 0 <= t < T

                def late(t, n):
                    return not isinstance(t, int) or t >= n

                def entry(eng, t, c, least, most):
                    return eng.value_load(tab[0:1, bass.ds(t, 1), c:c + 1].rearrange("p a b -> p (a b)"),
                                          min_val=least, max_val=most)

                def steps(eng, body, tail=None):
                    with eng.Fori(0, T) as t:
                        s0 = entry(eng, t, 0, 0, T * CH)
                        n = entry(eng, t, 1, 1, CH)
                        k0 = entry(eng, t, 2, 0, CH - 1)
                        with eng.Fori(0, n) as j:
                            body(t, s0 + j, k0 + j)
                        if tail:
                            tail(t)

                with nc.Block() as block:
                    @block.sync
                    def _(sp):
                        with sp.If(counted(sp) == 1):
                            def stage(t, r):
                                if is_tile(t):
                                    if late(t, RING):
                                        sp.wait_ge(strip_done, t - RING + 1)
                                    sp.dma_start(strips[:, r, :],
                                                 count_tab[bass.ds(t, 1), :, :].rearrange("a p m -> p (a m)"))\
                                      .then_inc(c_loaded[r], 16)
                            pipeline(sp, T, RING, RING, stage)
                        with sp.Else():
                            with sp.Fori(0, T) as t:
                                sp.wait_ge(whole_made, t + 1)
                                sp.dma_start(h_tab[bass.ds(t * P, P), :], row(state, t)).then_inc(h_stored, 16)

                    @block.tensor
                    def _(pe):
                        with pe.If(counted(pe) == 1):
                            def stage(t, r):
                                if is_tile(t):
                                    pe.wait_ge(c_loaded[r], (t - r) * (16 // RING) + 16)
                                    if late(t, RING):
                                        pe.wait_ge(both, t - RING + 1)
                                    nc.tensor.matmul(acc[r][:, :], ident_h[:, :], row(h_split, t), start=True, stop=False)
                                    for s in range(T):
                                        last = nc.tensor.matmul(acc[r][:, :], strips[:, r, s * P:(s + 1) * P],
                                                                h_split[:, s, :], start=False, stop=s == T - 1)
                                    last.then_inc(strip_done, 1)
                            pipeline(pe, T, RING, RING, stage)
                        with pe.Else():
                            def body(t, s, k):
                                pe.wait_ge(rows_ready, (s + 1) * 16)
                                pe.wait_ge(hot_ready, s + 1)
                                pe.wait_ge(free, s + 1)
                                nc.tensor.matmul(sum_ps[:, :], hot[:, :], rows[:, :], start=True, stop=True).then_inc(summed, 1)
                            steps(pe, body)

                    @block.scalar
                    def _(act):
                        with act.If(counted(act) == 1):
                            def stage(t, r):
                                if is_tile(t):
                                    act.wait_ge(strip_done, t + 1)
                                    if late(t, 2):
                                        act.wait_ge(both, t - 1)
                                    nc.scalar.activation(low[:, r % 2, :], acc[r][:, D:2 * D], ACT.Copy).then_inc(low_out, 1)
                            pipeline(act, T, RING, RING, stage)

                    @block.vector
                    def _(dve):
                        v = nc.vector
                        with dve.If(counted(dve) == 1):
                            def stage(t, r):
                                if is_tile(t):
                                    dve.wait_ge(low_out, t + 1)
                                    if late(t, 2):
                                        dve.wait_ge(biased, t - 1)
                                    v.tensor_tensor(total[:, r % 2, :], acc[r][:, 0:D], low[:, r % 2, :], ALU.add).then_inc(both, 1)
                                    dve.wait_ge(both, t + 1)
                                    v.scalar_tensor_tensor(row(state, t), total[:, r % 2, :], scale_down[:, i, bass.ds(t, 1)],
                                                           rows3[:, i, 0, :], ALU.mult, ALU.add).then_inc(biased, 1)
                                    dve.wait_ge(biased, t + 1)
                                    dve.sem_inc(seen, 1)
                                    v.bn_stats(row(stats6, t), row(state, t))
                            pipeline(dve, T, RING, RING, stage)
                        with dve.Else():
                            with dve.Fori(0, T) as t:
                                v.tensor_tensor(row(state, t), row(h_split, t)[:, 0:D], row(h_split, t)[:, D:2 * D],
                                                ALU.add).then_inc(whole_made, 1)
                            dve.wait_ge(whole_made, T)
                            dve.wait_ge(h_stored, 16 * T)
                            dve.sem_inc(free, 1)
                            v.tensor_copy(tile_iota[:, :], iota_row[:, :]).then_inc(iota_set, 1)
                            dve.wait_ge(iota_set, 1)

                            def body(t, s, k):
                                kk = nc.s_assert_within(k, 0, CH - 1)
                                v.tensor_scalar(hot[:, :], tile_iota[:, :], dst_col[:, bass.ds(kk, 1)], None,
                                                ALU.is_equal).then_inc(hot_ready, 1)
                                dve.wait_ge(summed, s + 1)
                                v.tensor_tensor(row(state, t), sum_ps[:, :], row(state, t), ALU.add).then_inc(free, 1)
                                dve.wait_ge(free, s + 2)

                            def tail(t):
                                v.tensor_scalar(tile_iota[:, :], tile_iota[:, :], float(P), None, ALU.add).then_inc(iota_set, 1)
                                dve.wait_ge(iota_set, t + 2)
                            steps(dve, body, tail)
                            with dve.Fori(0, T) as t:
                                v.scalar_tensor_tensor(row(state, t), row(state, t), scale_down[:, i, bass.ds(t, 1)],
                                                       rows3[:, i, 0, :], ALU.mult, ALU.add).then_inc(g_biased, 1)
                            dve.wait_ge(g_biased, T)
                            with dve.Fori(0, T) as t:
                                v.bn_stats(row(stats6, t), row(state, t))

                    @block.gpsimd
                    def _(pool):
                        with pool.If(counted(pool) == 0):
                            pool.wait_ge(h_stored, 16 * T)

                            def body(t, s, k):
                                kk = nc.s_assert_within(k, 0, CH - 1)
                                pool.wait_ge(free, s + 1)
                                nc.gpsimd.tensor_copy(idx[:, :], src_col[:, bass.ds(kk, 1)]).then_inc(idx_ready, 1)
                                pool.wait_ge(idx_ready, s + 1)
                                pool.sem_inc(idx_seen, 1)
                                nc.gpsimd.indirect_dma_start(rows[:, :], None, h_tab[:, :],
                                                             bass.IndirectOffsetOnAxis(idx[:, 0:1], 0)).then_inc(rows_ready, 16)
                            steps(pool, body)

        rstd_of_rows("x", 0)
        for i in range(L):
            layer_product(i)
            layer_sum(i)
            rstd_of_rows(f"l{i}", i + 1)
        h_stack.close()

        resid = sb(root, "resid", [P, T, D])
        w_scan = sb(root, "w_scan", [P, KC, D])
        b_scan = sb(root, "b_scan", [P, D])
        fin, x_again, x_zero, y_made = sem("fin"), sem("x_again"), sem("x_zero"), sem("y_made")
        with ExitStack() as ph:
            xr = sb(ph, "fin_x", [P, D])
            with nc.Block() as block:
                @block.sync
                def _(sp):
                    sp.wait_ge(x_zero, 1)
                    for g in range(G):
                        full = min((g + 1) * TS, T - 1)
                        sp.dma_start(resid[:, g * TS:full, :],
                                     x[g * TS * P:full * P, :].rearrange("(t p) d -> p t d", p=P)).then_inc(x_again, 16)
                    sp.dma_start(resid[0:LAST, T - 1, :], x[(T - 1) * P:N, :]).then_inc(x_again, 16)

                @block.vector
                def _(dve):
                    nc.vector.memset(resid[:, T - 1, :], 0.0).then_inc(x_zero, 1)
                    dve.wait_ge(x_again, 16 * (G + 1))
                    with dve.Fori(0, T) as t:
                        layer_input(dve, L, t, xr[:, :], fin, t * 5)
                        dve.wait_ge(fin, t * 5 + 4)
                        nc.vector.tensor_tensor(row(resid, t), row(resid, t), xr[:, :], ALU.add).then_inc(fin, 1)
                        dve.wait_ge(fin, t * 5 + 5)
                        dve.sem_inc(y_made, 1)
                        nc.vector.bn_stats(row(stats6, t), row(resid, t))
        rstd_of_rows("y", L + 1)
        with nc.Block() as block:
            @block.vector
            def _(dve):
                with dve.Fori(0, T) as t:
                    tt = bass.ds(t, 1)
                    nc.vector.tensor_scalar(row(state, t), row(resid, t), mv[:, tt, 0:1].rearrange("p a c -> p (a c)"),
                                            rstd[:, tt], ALU.subtract, ALU.mult)

        fw_loaded = sem("fw_loaded")
        fw_turned = sem("fw_turned")
        fw_dve = sem("fw_dve")
        fw_sum = sem("fw_sum")
        with ExitStack() as ph:
            w_nat = sb(ph, "w_nat", [P, KC, D])
            w_raw = sb(ph, "w_raw", [P, KC, D])
            w_scaled = sb(ph, "w_scaled", [P, KC, D])
            lnw = sb(ph, "lnw", [P, KC])
            lnb = sb(ph, "lnb", [P, KC])
            lnb_wide = sb(ph, "lnb_wide", [P, KC, P])
            mean_mat = sb(ph, "mean_mat", [P, P])
            fb = sb(ph, "fb", [P, D])
            wt_ps = ps(ph, "wt_ps", [P, KC, D])
            bias_ps = ps(ph, "bias_ps", [P, D])
            mean_ps = ps(ph, "mean_ps", [P, D])
            with nc.Block() as block:
                @block.sync
                def _(sp):
                    sp.dma_start(w_nat[:, :, :], ffn_w.rearrange("(k p) c -> p k c", p=P)).then_inc(fw_loaded, 16)
                    sp.dma_start(fb[:, :], ffn_b.partition_broadcast(P)).then_inc(fw_loaded, 16)
                    with nc.allow_non_contiguous_dma(reason="two vectors onto partitions"):
                        sp.dma_start(lnw[:, :], ffn_ln_w.rearrange("(k p) -> p k", p=P)).then_inc(fw_loaded, 16)
                        sp.dma_start(lnb[:, :], ffn_ln_b.rearrange("(k p) -> p k", p=P)).then_inc(fw_loaded, 16)

                @block.tensor
                def _(pe):
                    pe.wait_ge(fw_loaded, 64)
                    for c in range(KC):
                        for d in range(KC):
                            last = nc.tensor.transpose(wt_ps[:, c, d * P:(d + 1) * P], w_nat[:, d, c * P:(c + 1) * P], ident[:, :])
                    last.then_inc(fw_turned, 1)
                    pe.wait_ge(fw_dve, 3 + 2 * KC)
                    for c in range(KC):
                        nc.tensor.matmul(bias_ps[:, :], lnb_wide[:, c, :], w_raw[:, c, :], start=c == 0, stop=c == KC - 1)
                    for c in range(KC):
                        last = nc.tensor.matmul(mean_ps[:, :], mean_mat[:, :], w_scaled[:, c, :], start=c == 0, stop=c == KC - 1)
                    last.then_inc(fw_sum, 1)

                @block.vector
                def _(dve):
                    v = nc.vector
                    v.memset(mean_mat[:, :], 1.0 / D).then_inc(fw_dve, 1)
                    v.memset(lnb_wide[:, :, :], 1.0).then_inc(fw_dve, 1)
                    dve.wait_ge(fw_loaded, 64)
                    dve.wait_ge(fw_dve, 2)
                    dve.wait_ge(fw_turned, 1)
                    v.tensor_copy(w_raw[:, :, :], wt_ps[:, :, :]).then_inc(fw_dve, 1)
                    for c in range(KC):
                        v.tensor_scalar(lnb_wide[:, c, :], lnb_wide[:, c, :], lnb[:, c:c + 1], None, ALU.mult).then_inc(fw_dve, 1)
                        v.tensor_scalar(w_scaled[:, c, :], wt_ps[:, c, :], lnw[:, c:c + 1], None, ALU.mult).then_inc(fw_dve, 1)
                    dve.wait_ge(fw_dve, 3 + 2 * KC)
                    dve.wait_ge(fw_sum, 1)
                    for c in range(KC):
                        v.tensor_tensor(w_scan[:, c, :], w_scaled[:, c, :], mean_ps[:, :], ALU.subtract)
                    v.tensor_tensor(b_scan[:, :], fb[:, :], bias_ps[:, :], ALU.add)

        S = N_ITERS * G
        SLOTS = 4
        BANKS = -(-TS // 2)
        Z_LAG, TURN_LAG, VAR_LAG, PE_LAG, H_LAG = 0, 4, 3, 1, 5
        names = ("tanh_done", "h2_done", "sig_done", "z_done", "var_done", "rstd_done", "z_turned", "zt_copied",
                 "prod_done", "h_done", "var_ch")
        (tanh_done, h2_done, sig_done, z_done, var_done, rstd_done, z_turned, zt_copied, prod_done, h_done,
         var_ch) = (sem(s) for s in names)
        with ExitStack() as ph:
            h2 = sb(ph, "h2", [P, SLOTS, TS, D])
            z = sb(ph, "z", [P, SLOTS, TS, D])
            zt = sb(ph, "zt", [P, 2, TS * KC, P])
            zst = sb(ph, "zst", [P, TS, 6])
            zhalf = sb(ph, "zhalf", [P, TS])
            zsum = sb(ph, "zsum", [P, TS])
            zvar = sb(ph, "zvar", [P, 2, TS])
            zrs = sb(ph, "zrs", [P, SLOTS, TS])
            zt_ps = [ps(ph, f"zt_ps{j}", [P, 512]) for j in range(BANKS)]
            h_ps = [ps(ph, f"h_ps{j}", [P, 512]) for j in range(BANKS)]

            def tiles(j):
                return min(2, TS - 2 * j)

            def on(s):
                return not isinstance(s, int) or 0 <= s < S

            def late(s, n):
                return not isinstance(s, int) or s >= n

            with nc.Block() as block:
                @block.scalar
                def _(act):
                    def turn_out(s, u, j):
                        act.wait_ge(z_turned, s * BANKS + j + 1)
                        if late(s, 2):
                            act.wait_ge(prod_done, (s - 2) * BANKS + j + 1)
                        n = tiles(j) * D
                        nc.scalar.activation(zt[:, u, 4 * j:4 * j + 2 * tiles(j), :].rearrange("p a b -> p (a b)"),
                                             zt_ps[j][:, 0:n], ACT.Copy).then_inc(zt_copied, 1)

                    def stage(k, u):
                        if on(k):
                            if late(k, G):
                                act.wait_ge(h_done, (k - G + 1) * BANKS)
                            if late(k, SLOTS):
                                act.wait_ge(z_done, k - SLOTS + 1)
                            g = k % G
                            nc.scalar.activation(h2[:, u, :, :], state[:, bass.ds(g * TS, TS), :], ACT.Tanh).then_inc(tanh_done, 1)
                        s = k - TURN_LAG
                        if on(s):
                            for j in range(BANKS // 2):
                                turn_out(s, (u - TURN_LAG) % 2, j)
                        s = k - 2
                        if on(s):
                            act.wait_ge(h2_done, s + 1)
                            if late(s, SLOTS):
                                act.wait_ge(z_turned, (s - SLOTS + 1) * BANKS)
                                act.wait_ge(var_done, s - SLOTS + 1)
                            nc.scalar.activation(z[:, (u - 2) % SLOTS, :, :], h2[:, (u - 2) % SLOTS, :, :],
                                                 ACT.Sigmoid).then_inc(sig_done, 1)
                        s = k - TURN_LAG
                        if on(s):
                            for j in range(BANKS // 2, BANKS):
                                turn_out(s, (u - TURN_LAG) % 2, j)
                    pipeline(act, S, 8, SLOTS, stage)

                @block.vector
                def _(dve):
                    v = nc.vector

                    def stage(k, u):
                        s = k - 1
                        if on(s):
                            dve.wait_ge(tanh_done, s + 1)
                            w = (u - 1) % SLOTS
                            v.scalar_tensor_tensor(h2[:, w, :, :], h2[:, w, :, :], RES_SCALE,
                                                   state[:, bass.ds((s % G) * TS, TS), :], ALU.mult, ALU.add).then_inc(h2_done, 1)
                        s = k - H_LAG
                        if on(s):
                            dve.wait_ge(rstd_done, s + 1)
                            for j in range(BANKS):
                                dve.wait_ge(prod_done, s * BANKS + j + 1)
                                for a in range(tiles(j)):
                                    i = 2 * j + a
                                    last = v.scalar_tensor_tensor(
                                        state[:, bass.ds((s % G) * TS + i, 1), :].rearrange("p a d -> p (a d)"),
                                        h_ps[j][:, a * D:(a + 1) * D], zrs[:, (u - H_LAG) % SLOTS, i:i + 1], b_scan[:, :],
                                        ALU.mult, ALU.add)
                                last.then_inc(h_done, 1)
                        s = k - VAR_LAG
                        if on(s):
                            dve.wait_ge(z_done, s + 1)
                            for i in range(TS):
                                last = v.bn_stats(zst[:, i, :], z[:, (u - VAR_LAG) % SLOTS, i, :])
                            last.then_inc(var_ch, 1)
                            dve.wait_ge(var_ch, s * 4 + 1)
                            if late(s, 2):
                                dve.wait_ge(rstd_done, s - 1)
                            v.tensor_tensor(zhalf[:, :], zst[:, :, 1], zst[:, :, 4], ALU.subtract).then_inc(var_ch, 1)
                            v.scalar_tensor_tensor(zsum[:, :], zst[:, :, 2], D * EPS, zst[:, :, 5], ALU.add, ALU.add).then_inc(var_ch, 1)
                            dve.wait_ge(var_ch, s * 4 + 3)
                            v.scalar_tensor_tensor(zhalf[:, :], zhalf[:, :], 0.25, zhalf[:, :], ALU.mult, ALU.mult).then_inc(var_ch, 1)
                            dve.wait_ge(var_ch, s * 4 + 4)
                            v.scalar_tensor_tensor(zvar[:, (u - VAR_LAG) % 2, :], zsum[:, :], 1.0 / D, zhalf[:, :],
                                                   ALU.mult, ALU.add).then_inc(var_done, 1)
                    pipeline(dve, S, 8, SLOTS, stage)

                @block.gpsimd
                def _(pool):
                    def stage(k, u):
                        if on(k):
                            pool.wait_ge(sig_done, k + 1)
                            nc.gpsimd.tensor_tensor(z[:, u, :, :], h2[:, u, :, :], z[:, u, :, :], ALU.mult).then_inc(z_done, 1)
                        s = k - 1
                        if on(s):
                            pool.wait_ge(var_done, s + 1)
                            w = (u - 1) % SLOTS
                            if late(s, SLOTS):
                                pool.wait_ge(h_done, (s - SLOTS + 1) * BANKS)
                            nc.gpsimd.tensor_tensor(zrs[:, w, :], zvar[:, w % 2, :], neg_half[:, 0:TS], ALU.pow).then_inc(rstd_done, 1)
                    pipeline(pool, S, 8, SLOTS, stage)

                @block.tensor
                def _(pe):
                    def turn(s, u, j):
                        if late(s, 1):
                            pe.wait_ge(zt_copied, (s - 1) * BANKS + j + 1)
                        for a in range(tiles(j)):
                            for c in range(KC):
                                last = nc.tensor.transpose(zt_ps[j][:, (2 * a + c) * P:(2 * a + c + 1) * P],
                                                           z[:, u, 2 * j + a, c * P:(c + 1) * P], ident[:, :])
                        last.then_inc(z_turned, 1)

                    def multiply(s, u, j):
                        pe.wait_ge(zt_copied, s * BANKS + j + 1)
                        if late(s, 1):
                            pe.wait_ge(h_done, (s - 1) * BANKS + j + 1)
                        for a in range(tiles(j)):
                            for c in range(KC):
                                last = nc.tensor.matmul(h_ps[j][:, a * D:(a + 1) * D], zt[:, u, 4 * j + 2 * a + c, :],
                                                        w_scan[:, c, :], start=c == 0, stop=c == KC - 1)
                        last.then_inc(prod_done, 1)

                    def stage(k, u):
                        for j in range(BANKS):
                            if on(k):
                                if j == 0:
                                    pe.wait_ge(z_done, k + 1)
                                turn(k, u, j)
                            if on(k - PE_LAG):
                                multiply(k - PE_LAG, (u - PE_LAG) % 2, j)
                    pipeline(pe, S, 8, SLOTS, stage)

        out_made = sem("out_made")
        out_stored = sem("out_stored")
        with nc.Block() as block:
            @block.vector
            def _(dve):
                for g in range(G):
                    a = slice(g * TS, (g + 1) * TS)
                    nc.vector.tensor_tensor(state[:, a, :], state[:, a, :], resid[:, a, :], ALU.add).then_inc(out_made, 1)

            @block.sync
            def _(sp):
                for g in range(G):
                    sp.wait_ge(out_made, g + 1)
                    full = min((g + 1) * TS, T - 1)
                    sp.dma_start(out[g * TS * P:full * P, :].rearrange("(t p) d -> p t d", p=P),
                                 state[:, g * TS:full, :]).then_inc(out_stored, 16)
                sp.dma_start(out[(T - 1) * P:N, :], state[0:LAST, T - 1, :]).then_inc(out_stored, 16)
                sp.wait_ge(out_stored, 16 * (G + 1))


_INS = ["x", "src", "dst", "L0_gnn_W", "L0_gnn_b", "L0_gnn_gamma", "L0_gnn_beta",
        "L0_ffn_ln_w", "L0_ffn_ln_b", "L0_ffn_W", "L0_ffn_b"]


def kernel(**inputs):
    import numpy as _np
    import concourse.bacc as _bacc
    from concourse import mybir as _mybir
    from concourse.bass_utils import run_bass_kernel_spmd as _run

    nc = _bacc.Bacc("TRN2", target_bir_lowering=False, num_devices=1)
    arrays, args = {}, []
    for name in _INS:
        a = _np.ascontiguousarray(inputs[name])
        arrays[f"in_{name}_dram"] = a
        args.append(nc.dram_tensor(f"in_{name}_dram", a.shape, _mybir.dt.from_np(a.dtype), kind="ExternalInput").ap())
    shape = tuple(_np.shape(inputs["x"]))
    args.append(nc.dram_tensor("out_0_dram", shape, _mybir.dt.float32, kind="ExternalOutput").ap())
    build_gnn_ffn(nc, *args)
    r = _run(nc, [arrays], core_ids=[0])
    return r.results[0]["out_0_dram"]
```

```python
import concourse.bass as bass
from concourse import mybir
from contextlib import ExitStack, nullcontext

P = 128
F32 = mybir.dt.float32
F16 = mybir.dt.float16
I32 = mybir.dt.int32
ALU = mybir.AluOpType
ACT = mybir.ActivationFunctionType
AX = mybir.AxisListType

EPS = 1e-5
RES_SCALE = 0.01
N_ITERS = 30
NO_NODE = 1 << 20

TS = 7

WIN = 6
WC = 2
SP_WINDOWS = 14
GW = 2
RING = 4
F16_TOP = 2.0 ** 14


def pipeline(eng, slots, depth, unroll, stage):
    assert depth % unroll == 0
    body = (slots - depth) // unroll
    for k in range(depth):
        stage(k, k % unroll)
    with eng.Fori(0, body) as m:
        for u in range(unroll):
            stage(m * unroll + (depth + u), u)
    for k in range(depth + body * unroll, slots + depth):
        stage(k, k % unroll)


def build_gnn_ffn(nc, x, src, dst, gnn_w, gnn_b, gnn_gamma, gnn_beta, ffn_ln_w, ffn_ln_b, ffn_w, ffn_b, out):
    N, D = x.shape
    E = src.shape[0]
    L = gnn_w.shape[0]
    KC = D // P
    T = -(-N // P)
    LAST = N - (T - 1) * P
    CB = -(-E // (P * P))
    CH = CB * P
    FULL_CB = E // (P * P)
    FULL_ROWS = (E - FULL_CB * P * P) // P
    REST = E % P
    G = T // TS
    assert G * TS == T
    WPT = -(-P // WIN)
    W_ALL = T * WPT
    WP = 98
    WG = W_ALL // WP
    assert WP * WG == W_ALL
    NG = WPT // GW
    GC = GW * WC
    assert NG * GW == WPT and NG % 2 == 1
    KEYS = WIN * T

    root = ExitStack()
    with root:
        def sem(name):
            return root.enter_context(nc.semaphore(name))

        def sb(stack, name, shape, dt=F32):
            return stack.enter_context(nc.sbuf_tensor(name, shape, dt))

        def ps(stack, name, shape, dt=F32):
            return stack.enter_context(nc.psum_tensor(name, shape, dt))

        def dram(name, shape, dt):
            return nc.dram_tensor(name, shape, dt, kind="Internal").ap()

        def row(buf, t):
            return buf[:, bass.ds(t, 1), :].rearrange("p a d -> p (a d)")

        state = sb(root, "state", [P, T, D])
        mv = sb(root, "mv", [P, T, 2])
        rstd = sb(root, "rstd", [P, T])
        neg_half = sb(root, "neg_half", [P, T])
        ident = sb(root, "ident", [P, P])
        w_scan = sb(root, "w_scan", [P, KC, D])
        b_scan = sb(root, "b_scan", [P, D])
        flag = sb(root, "flag", [1, 1], I32)

        key_tab = dram("key_tab", [CH * P, 2], F32)
        dst_tab = dram("dst_tab", [CH, P], F32)
        src_tab = dram("src_tab", [CH, P], F32)
        most_tab = dram("chunk_most", [CB, P], F32)
        least_tab = dram("chunk_least", [CB, P], F32)
        base_tab = dram("window_base", [W_ALL], F32)
        start_tab = dram("window_start", [W_ALL], I32)
        count_tab = dram("count_tab", [T, P, T * P], F16)
        range_tab = dram("range_tab", [T, 2], F32)
        h_tab = dram("h_tab", [T * P, D], F32)

        gnn = root.enter_context(ExitStack())
        dinv = sb(gnn, "dinv", [P, T])
        degs = sb(gnn, "degs", [P, T])
        scale_up = sb(gnn, "scale_up", [P, L, T])
        scale_down = sb(gnn, "scale_down", [P, L, T])
        sigma = sb(gnn, "sigma", [P, L, 2])
        iota_row = sb(gnn, "iota_row", [P, P])
        iota_h = sb(gnn, "iota_h", [P, KEYS], F16)
        iota_g = sb(gnn, "iota_g", [P, KEYS, GC], F16)
        iota_part = sb(gnn, "iota_part", [P, 1])
        ones_h = sb(gnn, "ones_h", [P, 1], F16)
        half_tile = sb(gnn, "half_tile", [P, 2, L])
        ones_f = sb(gnn, "ones_f", [P, P])
        stats6 = sb(gnn, "stats6", [P, T, 6])
        w_gnn = sb(gnn, "w_gnn", [P, L, KC, D])
        cols2 = sb(gnn, "cols2", [P, L, 2, KC])
        rows3 = sb(gnn, "rows3", [P, L, 3, D])

        x_loaded, edges_loaded, params_loaded = sem("x_loaded"), sem("edges_loaded"), sem("params_loaded")
        pad_set, const_set = sem("pad_set"), sem("const_set")
        keys_stored, dst_stored, base_stored, wide_made, most_turned = (
            sem(s) for s in ("keys_stored", "dst_stored", "base_stored", "wide_made", "most_turned"))
        part_done, key_done, minmax_done, tabs_stored = sem("part_done"), sem("key_done"), sem("minmax_done"), sem("tabs_stored")
        base_made = sem("base_made")
        thr_loaded, find, idx_made, rows_got, start_stored, start_loaded = (
            sem(s) for s in ("thr_loaded", "find", "idx_made", "rows_got", "start_stored", "start_loaded"))
        bound, bound_pe, bound_pool = sem("bound"), sem("bound_pe"), sem("bound_pool")
        fw_loaded, fw_turned, fw_dve, fw_sum = (sem(s) for s in ("fw_loaded", "fw_turned", "fw_dve", "fw_sum"))
        starts = sb(gnn, "starts", [1, W_ALL], I32)

        early = gnn.enter_context(ExitStack())
        with nullcontext(early) as ph:
            dst_nat = sb(ph, "dst_nat", [P, CB, P], I32)
            src_nat = sb(ph, "src_nat", [P, CB, P], I32)
            src_part = sb(ph, "src_part", [P, 2, CB, P], I32)
            dst_f = sb(ph, "dst_f", [P, CB, P])
            src_f = sb(ph, "src_f", [P, CB, P])
            tile_f = sb(ph, "tile_f", [P, CB, P])
            keys = sb(ph, "keys", [P, CB, P, 2])
            tmin = sb(ph, "tmin", [P, CB])
            tmax = sb(ph, "tmax", [P, CB])
            w_base = sb(ph, "w_base", [T, WPT])
            thr = sb(ph, "thr", [WP, WG])
            w_nat = sb(ph, "w_nat", [P, KC, D])
            lnw = sb(ph, "lnw", [P, KC])
            lnb = sb(ph, "lnb", [P, KC])
            fb = sb(ph, "fb", [P, D])
            with nc.Block() as block:
                @block.sync
                def _(sp):
                    n_full = FULL_CB * P * P
                    n_rows = n_full + FULL_ROWS * P
                    for i, (nat, e) in enumerate(((dst_nat, dst), (src_nat, src))):
                        sp.dma_start(nat[:, 0:FULL_CB, :],
                                     e[0:n_full].rearrange("(b p e) -> p b e", p=P, e=P)).then_inc(edges_loaded, 16)
                        sp.wait_ge(pad_set, i + 1)
                        sp.dma_start(nat[0:FULL_ROWS, FULL_CB, :],
                                     e[n_full:n_rows].rearrange("(p e) -> p e", e=P)).then_inc(edges_loaded, 16)
                        sp.dma_start(nat[FULL_ROWS:FULL_ROWS + 1, FULL_CB, 0:REST],
                                     e[n_rows:E].rearrange("(p e) -> p e", p=1)).then_inc(edges_loaded, 16)
                    sp.wait_ge(part_done, 1)
                    sp.dma_start(dst_tab.rearrange("(b p) e -> p b e", p=P), dst_f[:, :, :]).then_inc(dst_stored, 16)
                    with nc.allow_non_contiguous_dma(reason="two small tables"):
                        sp.wait_ge(minmax_done, 1)
                        sp.dma_start(most_tab.rearrange("b p -> p b"), tmax[:, :]).then_inc(tabs_stored, 16)
                        sp.wait_ge(minmax_done, 2)
                        sp.dma_start(least_tab.rearrange("b p -> p b"), tmin[:, :]).then_inc(tabs_stored, 16)
                    sp.wait_ge(part_done, 2)
                    sp.dma_start(src_tab.rearrange("(b p) e -> p b e", p=P), src_f[:, :, :]).then_inc(keys_stored, 16)
                    sp.wait_ge(key_done, 2)
                    sp.dma_start(key_tab.rearrange("(b p e) c -> p b (e c)", p=P, e=P),
                                 keys[:, :, :, :].rearrange("p b e c -> p b (e c)")).then_inc(keys_stored, 16)
                    sp.dma_start(state[:, 0:T - 1, :],
                                 x[0:(T - 1) * P, :].rearrange("(t p) d -> p t d", p=P)).then_inc(x_loaded, 16)
                    sp.wait_ge(pad_set, 3)
                    sp.dma_start(state[0:LAST, T - 1, :], x[(T - 1) * P:N, :]).then_inc(x_loaded, 16)

                @block.scalar
                def _(act):
                    act.wait_ge(base_made, 1)
                    act.dma_start(base_tab.rearrange("(t j) -> t j", t=T), w_base[:, :]).then_inc(base_stored, 16)
                    act.wait_ge(base_stored, 16)
                    act.dma_start(thr[:, :], base_tab.rearrange("(p g) -> p g", g=WG)).then_inc(thr_loaded, 16)
                    for i in range(L):
                        act.dma_start(w_gnn[:, i, :, :],
                                      gnn_w[i, :, :].rearrange("(k p) d -> p k d", p=P)).then_inc(params_loaded, 16)
                        for j, v in enumerate((gnn_b, gnn_gamma, gnn_beta)):
                            act.dma_start(rows3[:, i, j, :],
                                          v[i:i + 1, :].partition_broadcast(P)).then_inc(params_loaded, 16)
                        with nc.allow_non_contiguous_dma(reason="two vectors onto partitions"):
                            for j, v in enumerate((gnn_gamma, gnn_beta)):
                                act.dma_start(cols2[:, i, j, :],
                                              v[i, :].rearrange("(k p) -> p k", p=P)).then_inc(params_loaded, 16)
                    act.dma_start(w_nat[:, :, :], ffn_w.rearrange("(k p) c -> p k c", p=P)).then_inc(fw_loaded, 16)
                    act.dma_start(fb[:, :], ffn_b.partition_broadcast(P)).then_inc(fw_loaded, 16)
                    with nc.allow_non_contiguous_dma(reason="two vectors onto partitions"):
                        act.dma_start(lnw[:, :], ffn_ln_w.rearrange("(k p) -> p k", p=P)).then_inc(fw_loaded, 16)
                        act.dma_start(lnb[:, :], ffn_ln_b.rearrange("(k p) -> p k", p=P)).then_inc(fw_loaded, 16)
                    act.wait_ge(params_loaded, 16 * 6 * L)

                @block.gpsimd
                def _(pool):
                    g = nc.gpsimd
                    g.iota(w_base[:, :], [[WIN, WPT]], base=0, channel_multiplier=P,
                           allow_small_or_imprecise_dtypes=True).then_inc(base_made, 1)
                    g.iota(iota_row[:, :], [[1, P]], base=0, channel_multiplier=0, allow_small_or_imprecise_dtypes=True)
                    g.iota(iota_h[:, :], [[1, KEYS]], base=0, channel_multiplier=0, allow_small_or_imprecise_dtypes=True)
                    g.iota(iota_g[:, :, :], [[1, KEYS], [0, GC]], base=0, channel_multiplier=0, allow_small_or_imprecise_dtypes=True)
                    g.iota(iota_part[:, :], [[0, 1]], base=0, channel_multiplier=1, allow_small_or_imprecise_dtypes=True)
                    g.memset(neg_half[:, :], -0.5)
                    g.memset(half_tile[:, :, :], 0.5)
                    g.memset(ones_h[:, :], 1.0)
                    g.memset(ones_f[:, :], 1.0)
                    g.memset(ident[:, :], 0.0).then_inc(const_set, 1)
                    pool.wait_ge(const_set, 1)
                    g.affine_select(out=ident[:, :], in_=ident[:, :], compare_op=ALU.not_equal, fill=1.0,
                                    base=0, pattern=[[-1, P]], channel_multiplier=1).then_inc(const_set, 1)

                @block.vector
                def _(dve):
                    v = nc.vector
                    v.memset(dst_nat[:, FULL_CB, :], NO_NODE).then_inc(pad_set, 1)
                    v.memset(src_nat[:, FULL_CB, :], 0).then_inc(pad_set, 1)
                    v.memset(state[:, T - 1, :], 0.0).then_inc(pad_set, 1)
                    dve.wait_ge(edges_loaded, 96)
                    v.tensor_copy(dst_f[:, :, :], dst_nat[:, :, :]).then_inc(part_done, 1)
                    dve.wait_ge(part_done, 1)
                    v.tensor_reduce(tmax[:, :], dst_f[:, :, :], AX.X, ALU.max).then_inc(minmax_done, 1)
                    v.tensor_reduce(tmin[:, :], dst_f[:, :, :], AX.X, ALU.min).then_inc(minmax_done, 1)
                    v.tensor_copy(src_f[:, :, :], src_nat[:, :, :]).then_inc(part_done, 1)
                    v.tensor_scalar(src_part[:, 1, :, :], src_nat[:, :, :], P - 1, None, ALU.bitwise_and)
                    v.tensor_scalar(src_part[:, 0, :, :], src_nat[:, :, :], P.bit_length() - 1, None,
                                    ALU.arith_shift_right).then_inc(part_done, 1)
                    dve.wait_ge(part_done, 3)
                    v.tensor_copy(keys[:, :, :, 1], src_part[:, 1, :, :]).then_inc(key_done, 1)
                    v.tensor_copy(tile_f[:, :, :], src_part[:, 0, :, :]).then_inc(part_done, 1)
                    dve.wait_ge(part_done, 4)
                    v.scalar_tensor_tensor(keys[:, :, :, 0], dst_f[:, :, :], float(T), tile_f[:, :, :],
                                           ALU.mult, ALU.add).then_inc(key_done, 1)

        with ExitStack() as ph:
            wide = sb(ph, "wide", [P, CB, WP])
            most_ps = ps(ph, "most_ps", [P, CH])
            junk = sb(ph, "junk", [P, CH])
            whole = sb(ph, "whole", [WP, WG])
            rest = sb(ph, "rest", [WP, WG])
            start_f = sb(ph, "start_f", [WP, WG])
            idx = sb(ph, "idx", [WP, WG], I32)
            start_i = sb(ph, "start_i", [WP, WG], I32)
            got = sb(ph, "got", [WP, WG, P])
            wsum = sb(ph, "wsum", [P, L])
            bsum = sb(ph, "bsum", [P, L])
            gmax = sb(ph, "gmax", [P, L])
            sq = sb(ph, "sq", [P, KC * D])
            norm = sb(ph, "norm", [P, 2, L])
            xnorm = sb(ph, "xnorm", [P, L])
            wsum_ps = ps(ph, "wsum_ps", [P, L])
            w_raw = sb(ph, "w_raw", [P, KC, D])
            w_scaled = sb(ph, "w_scaled", [P, KC, D])
            lnb_wide = sb(ph, "lnb_wide", [P, KC, P])
            mean_mat = sb(ph, "mean_mat", [P, P])
            wt_ps = ps(ph, "wt_ps", [P, KC, D])
            bias_ps = ps(ph, "bias_ps", [P, 2, D])
            with nc.Block() as block:
                @block.sync
                def _(sp):
                    sp.wait_ge(tabs_stored, 32)
                    sp.wait_ge(keys_stored, 32)

                @block.scalar
                def _(act):
                    act.wait_ge(find, 2 * WG + 3)
                    act.dma_start(start_tab.rearrange("(p g) -> p g", g=WG), start_i[:, :]).then_inc(start_stored, 16)
                    act.wait_ge(start_stored, 16)
                    act.dma_start(starts[:, :], start_tab.rearrange("(a w) -> a w", a=1)).then_inc(start_loaded, 16)
                    act.wait_ge(start_loaded, 16)

                @block.gpsimd
                def _(pool):
                    pool.wait_ge(dst_stored, 16)
                    pool.wait_ge(idx_made, 1)
                    for g in range(WG):
                        nc.gpsimd.indirect_dma_start(got[:, g, :], None, dst_tab[:, :],
                                                     bass.IndirectOffsetOnAxis(idx[:, g:g + 1], 0)).then_inc(rows_got, 16)
                    pool.wait_ge(bound, 3 * L + 2)
                    nc.gpsimd.tensor_tensor(norm[:, :, :], norm[:, :, :], half_tile[:, :, :], ALU.pow).then_inc(bound_pool, 1)

                @block.tensor
                def _(pe):
                    pe.wait_ge(wide_made, 1)
                    for b in range(CB):
                        last = nc.tensor.matmul(most_ps[0:WP, b * P:(b + 1) * P], wide[:, b, :], ident[:, :], start=True, stop=True)
                    last.then_inc(most_turned, 1)
                    pe.wait_ge(bound, L)
                    nc.tensor.matmul(wsum_ps[:, :], ones_f[:, :], wsum[:, :], start=True, stop=True).then_inc(bound_pe, 1)
                    pe.wait_ge(fw_loaded, 64)
                    for c in range(KC):
                        for d in range(KC):
                            last = nc.tensor.transpose(wt_ps[:, c, d * P:(d + 1) * P], w_nat[:, d, c * P:(c + 1) * P], ident[:, :])
                    last.then_inc(fw_turned, 1)
                    pe.wait_ge(fw_dve, 3 + 2 * KC)
                    for c in range(KC):
                        nc.tensor.matmul(bias_ps[:, 0, :], lnb_wide[:, c, :], w_raw[:, c, :], start=c == 0, stop=c == KC - 1)
                    for c in range(KC):
                        last = nc.tensor.matmul(bias_ps[:, 1, :], mean_mat[:, :], w_scaled[:, c, :], start=c == 0, stop=c == KC - 1)
                    last.then_inc(fw_sum, 1)

                @block.vector
                def _(dve):
                    v = nc.vector
                    v.tensor_copy(wide[:, :, :], tmax[:, :].unsqueeze(2).to_broadcast([P, CB, WP])).then_inc(wide_made, 1)
                    dve.wait_ge(most_turned, 1)
                    dve.wait_ge(thr_loaded, 16)
                    for g in range(WG):
                        if g >= 1:
                            dve.wait_ge(find, g)
                        v.tensor_scalar(junk[0:WP, :], most_ps[0:WP, :], thr[:, g:g + 1], None, ALU.is_lt, ALU.add,
                                        accum_out=whole[:, g:g + 1]).then_inc(find, 1)
                    dve.wait_ge(find, WG)
                    v.tensor_copy(idx[:, :], whole[:, :]).then_inc(idx_made, 1)
                    for i in range(L):
                        if i >= 1:
                            dve.wait_ge(bound, i)
                        v.tensor_tensor_reduce(out=sq[:, :], in0=w_gnn[:, i, :, :].rearrange("p k d -> p (k d)"),
                                               in1=w_gnn[:, i, :, :].rearrange("p k d -> p (k d)"), scale=1.0, scalar=0.0,
                                               op0=ALU.mult, op1=ALU.add, accum_out=wsum[:, i:i + 1]).then_inc(bound, 1)
                    for i in range(L):
                        dve.wait_ge(bound, L + 2 * i)
                        v.tensor_tensor_reduce(out=sq[:, 0:D], in0=rows3[:, i, 2, :], in1=rows3[:, i, 2, :], scale=1.0,
                                               scalar=0.0, op0=ALU.mult, op1=ALU.add,
                                               accum_out=bsum[:, i:i + 1]).then_inc(bound, 1)
                        v.tensor_reduce(gmax[:, i:i + 1], rows3[:, i, 1, :], AX.X, ALU.max,
                                        apply_absolute_value=True).then_inc(bound, 1)
                    dve.wait_ge(bound, 3 * L)
                    v.tensor_copy(norm[:, 1, :], bsum[:, :]).then_inc(bound, 1)
                    dve.wait_ge(bound_pe, 1)
                    v.tensor_copy(norm[:, 0, :], wsum_ps[:, :]).then_inc(bound, 1)
                    dve.wait_ge(bound_pool, 1)
                    n = [3 * L + 2]

                    def link(ins):
                        n[0] += 1
                        ins.then_inc(bound, 1)
                        dve.wait_ge(bound, n[0])
                    link(v.memset(xnorm[:, 0:1], float(D) ** 0.5))
                    link(v.scalar_tensor_tensor(xnorm[:, 1:L], gmax[:, 0:L - 1], float(D) ** 0.5, norm[:, 1, 0:L - 1],
                                                ALU.mult, ALU.add))
                    link(v.tensor_tensor(xnorm[:, :], xnorm[:, :], norm[:, 0, :], ALU.mult))
                    link(v.tensor_scalar(xnorm[:, :], xnorm[:, :], 1e-30, 1.0 / F16_TOP, ALU.max, ALU.mult))
                    v.tensor_copy(sigma[:, :, 1], xnorm[:, :])
                    link(v.reciprocal(sigma[:, :, 0], xnorm[:, :]))
                    v.memset(mean_mat[:, :], 1.0 / D).then_inc(fw_dve, 1)
                    v.memset(lnb_wide[:, :, :], 1.0).then_inc(fw_dve, 1)
                    dve.wait_ge(fw_loaded, 64)
                    dve.wait_ge(fw_dve, 2)
                    dve.wait_ge(fw_turned, 1)
                    v.tensor_copy(w_raw[:, :, :], wt_ps[:, :, :]).then_inc(fw_dve, 1)
                    for c in range(KC):
                        v.tensor_scalar(lnb_wide[:, c, :], lnb_wide[:, c, :], lnb[:, c:c + 1], None, ALU.mult).then_inc(fw_dve, 1)
                        v.tensor_scalar(w_scaled[:, c, :], wt_ps[:, c, :], lnw[:, c:c + 1], None, ALU.mult).then_inc(fw_dve, 1)
                    dve.wait_ge(fw_dve, 3 + 2 * KC)
                    dve.wait_ge(fw_sum, 1)
                    for c in range(KC):
                        v.tensor_tensor(w_scan[:, c, :], w_scaled[:, c, :], bias_ps[:, 1, :], ALU.subtract)
                    v.tensor_tensor(b_scan[:, :], fb[:, :], bias_ps[:, 0, :], ALU.add)
                    dve.wait_ge(x_loaded, 32)
                    for t in range(T):
                        v.bn_stats(stats6[:, t, :], state[:, t, :])
                    for g in range(WG):
                        dve.wait_ge(rows_got, 16 * WG)
                        dve.wait_ge(find, WG + g)
                        v.tensor_scalar(junk[0:WP, 0:P], got[:, g, :], thr[:, g:g + 1], None, ALU.is_lt, ALU.add,
                                        accum_out=rest[:, g:g + 1]).then_inc(find, 1)
                    dve.wait_ge(find, 2 * WG)
                    v.scalar_tensor_tensor(start_f[:, :], whole[:, :], float(P), rest[:, :], ALU.mult, ALU.add).then_inc(find, 1)
                    dve.wait_ge(find, 2 * WG + 1)
                    v.tensor_copy(start_i[:, :], start_f[:, :]).then_inc(find, 1)
                    dve.wait_ge(find, 2 * WG + 2)
                    dve.sem_inc(find, 1)

        early.close()

        def counted(eng):
            return eng.value_load(flag[0:1, 0:1], min_val=0, max_val=1)

        stat_steps, stat_steps_only, rstd_ready = sem("stat_steps"), sem("stat_steps_only"), sem("rstd_ready")
        def only(eng, always):
            return nullcontext() if always else eng.If(counted(eng) == 0)

        def rstd_of_rows(name, turn, always=True):
            small, base = stat_steps if always else stat_steps_only, 7 * turn
            with ExitStack() as ph:
                half = sb(ph, f"{name}_half", [P, T])
                with nc.Block() as block:
                    @block.vector
                    def _(dve):
                        with only(dve, always):
                            v = nc.vector
                            v.tensor_tensor(mv[:, :, 0], stats6[:, :, 1], stats6[:, :, 4], ALU.add).then_inc(small, 1)
                            v.tensor_tensor(half[:, :], stats6[:, :, 1], stats6[:, :, 4], ALU.subtract).then_inc(small, 1)
                            v.tensor_tensor(mv[:, :, 1], stats6[:, :, 2], stats6[:, :, 5], ALU.add).then_inc(small, 1)
                            dve.wait_ge(small, base + 3)
                            v.tensor_scalar(mv[:, :, 0], mv[:, :, 0], 0.5, None, ALU.mult).then_inc(small, 1)
                            v.scalar_tensor_tensor(half[:, :], half[:, :], 0.25, half[:, :], ALU.mult, ALU.mult).then_inc(small, 1)
                            v.tensor_scalar(mv[:, :, 1], mv[:, :, 1], 1.0 / D, EPS, ALU.mult, ALU.add).then_inc(small, 1)
                            dve.wait_ge(small, base + 6)
                            v.tensor_tensor(mv[:, :, 1], mv[:, :, 1], half[:, :], ALU.add).then_inc(small, 1)

                    @block.gpsimd
                    def _(pool):
                        with only(pool, always):
                            pool.wait_ge(small, base + 7)
                            nc.gpsimd.tensor_tensor(rstd[:, :], mv[:, :, 1], neg_half[:, :], ALU.pow).then_inc(rstd_ready, 1)

        xr_made, y_made = sem("xr_made"), sem("y_made")
        x_made, x_turned, xt_copied, prod, hi_made, lo_made, dch = (
            sem(s) for s in ("x_made", "x_turned", "xt_copied", "prod", "hi_made", "lo_made", "input_steps"))

        rstd_of_rows("x", 0)
        h_stack = gnn.enter_context(ExitStack())
        h_split = sb(h_stack, "h_split", [P, T, 2 * D], F16)

        ev_loaded = [sem(f"ev_loaded{u}") for u in range(2)]
        ev_loaded_pool = [sem(f"ev_loaded_pool{u}") for u in range(2)]
        strip_stored = [sem(f"strip_stored{u}") for u in range(2)]
        PAIRS = -(-NG // 2)
        keys_made, src_made, tile_ch, tile_scale = (sem(s) for s in ("keys_made", "src_made", "tile_ch", "tile_scale"))
        hots_made, win_done, win_out, deg_made, deg_out, base_ch = (
            sem(s) for s in ("hots_made", "win_done", "win_out", "deg_made", "deg_out", "base_ch"))
        with ExitStack() as ph:
            ev = sb(ph, "ev", [P, 2, WPT, WC, 2])
            key_rel = sb(ph, "key_rel", [P, 2, WPT, WC], F16)
            key_f = sb(ph, "key_f", [P, WPT, WC])
            src_row = sb(ph, "src_row", [P, 2, WPT, WC], F16)
            first_key = sb(ph, "first_key", [P, WPT])
            hot_key = sb(ph, "hot_key", [P, NG, KEYS, GC], F16)
            hot_src = sb(ph, "hot_src", [P, 2, NG, P, GC], F16)
            strip = sb(ph, "strip", [P, 2, T, P], F16)
            win_ps = [ps(ph, f"win_ps{i}", [P, GW, 512]) for i in range(2)]
            xr = sb(ph, "c_xr", [P, 2, D])
            xt = sb(ph, "c_xt", [P, 2, KC, P])
            deg1 = sb(ph, "deg1", [P, T])
            xt_ps = ps(ph, "c_xt_ps", [P, 512])
            h_ps = ps(ph, "c_h_ps", [P, 512])
            deg_ps = [ps(ph, f"deg_ps{i}", [P, 512]) for i in range(2)]

            with nc.Block() as block:
                def is_tile(t):
                    return not isinstance(t, int) or 0 <= t < T

                def late(t, n):
                    return not isinstance(t, int) or t >= n

                def load_edges(eng, engine_type, loaded, k, u, windows):
                    if late(k, 2):
                        eng.wait_ge(keys_made, (k - 1) * 3)
                    _, first_edges = nc.values_load_multi_w_load_instructions(
                        starts[0:1, bass.ds(k * WPT + windows[0], len(windows))], engines=(engine_type,), min_val=0,
                        max_val=E, skip_runtime_bounds_check_because="a count of edges, so at most E")
                    for j, e0 in zip(windows, first_edges):
                        eng.dma_start(ev[:, u, j, :, :].rearrange("p c k -> p (c k)"),
                                      key_tab[bass.ds(e0, WC * P), :].rearrange("(p c) k -> p (c k)", c=WC))\
                           .then_inc(loaded[u], 16)

                @block.sync
                def _(sp):
                    def stage(k, u):
                        if is_tile(k):
                            load_edges(sp, mybir.EngineType.SP, ev_loaded, k, u, range(0, 8))
                            load_edges(sp, mybir.EngineType.SP, ev_loaded, k, u, range(8, SP_WINDOWS))
                    pipeline(sp, T, 2, 2, stage)
                    sp.wait_ge(strip_stored[0], 16 * ((T + 1) // 2))
                    sp.wait_ge(strip_stored[1], 16 * (T // 2))

                @block.gpsimd
                def _(pool):
                    def stage(k, u):
                        if is_tile(k):
                            load_edges(pool, mybir.EngineType.Pool, ev_loaded_pool, k, u, range(SP_WINDOWS, WPT))
                        t = k - 3
                        if is_tile(t):
                            tt = bass.ds(t, 1)
                            pool.wait_ge(deg_out, t + 1)
                            nc.gpsimd.tensor_tensor(deg1[:, tt], degs[:, tt], ones_f[:, 0:1], ALU.add).then_inc(tile_ch, 1)
                            pool.wait_ge(tile_ch, 2 * t + 1)
                            nc.gpsimd.tensor_tensor(dinv[:, tt], deg1[:, tt], neg_half[:, 0:1], ALU.pow).then_inc(tile_ch, 1)
                            pool.wait_ge(tile_ch, 2 * t + 2)
                            nc.gpsimd.tensor_tensor(scale_up[:, 0, tt], dinv[:, tt], sigma[:, 0, 0:1], ALU.mult).then_inc(tile_scale, 1)
                    pipeline(pool, T, 4, 2, stage)

                @block.vector
                def _(dve):
                    v = nc.vector
                    v.tensor_scalar(first_key[:, :], iota_row[:, 0:WPT], float(WIN * T), None, ALU.mult).then_inc(base_ch, 1)

                    def in_groups(buf, u, g, n, rows):
                        return buf[:, u, g * GW:(g + n) * GW, :].rearrange("p (g j) c -> p g (j c)", j=GW)\
                            .unsqueeze(2).to_broadcast([P, n, rows, GC])

                    def stage(k, u):
                        t = k - 4
                        if is_tile(t):
                            dve.wait_ge(hi_made, t + 1)
                            v.scalar_tensor_tensor(row(h_split, t)[:, D:2 * D], h_ps[:, 0:D], scale_up[:, 0, bass.ds(t, 1)],
                                                   row(h_split, t)[:, 0:D], ALU.mult, ALU.subtract).then_inc(lo_made, 1)
                        if not is_tile(k):
                            return
                        if late(k, 2):
                            dve.wait_ge(x_turned, k - 1)
                        v.tensor_scalar(xr[:, u, :], row(state, k), mv[:, bass.ds(k, 1), 0:1].rearrange("p a c -> p (a c)"),
                                        rstd[:, bass.ds(k, 1)], ALU.subtract, ALU.mult).then_inc(x_made, 1)
                        dve.wait_ge(ev_loaded[u], (k - u) * (8 * SP_WINDOWS) + 16 * SP_WINDOWS)
                        dve.wait_ge(ev_loaded_pool[u], (k - u) * (8 * (WPT - SP_WINDOWS)) + 16 * (WPT - SP_WINDOWS))
                        dve.wait_ge(base_ch, k + 1)
                        v.tensor_tensor(key_f[:, :, :], ev[:, u, :, :, 0],
                                        first_key[:, :].unsqueeze(2).to_broadcast([P, WPT, WC]), ALU.subtract).then_inc(keys_made, 1)
                        dve.wait_ge(keys_made, 3 * k + 1)
                        v.tensor_scalar(key_rel[:, u, :, :], key_f[:, :, :], -1.0, float(KEYS), ALU.max, ALU.min).then_inc(keys_made, 1)
                        v.tensor_copy(src_row[:, u, :, :], ev[:, u, :, :, 1]).then_inc(keys_made, 1)
                        dve.wait_ge(keys_made, 3 * k + 3)
                        v.tensor_scalar(first_key[:, :], first_key[:, :], float(P * T), None, ALU.add).then_inc(base_ch, 1)
                        v.tensor_tensor(hot_src[:, u, :, :, :], iota_g[:, 0:P, :].unsqueeze(1).to_broadcast([P, NG, P, GC]),
                                        in_groups(src_row, u, 0, NG, P), ALU.is_equal).then_inc(src_made, 1)
                        for g in range(0, NG, 2):
                            n = min(2, NG - g)
                            if late(k, 1):
                                dve.wait_ge(win_done, (k - 1) * NG + g + n)
                            v.tensor_tensor(hot_key[:, g:g + n, :, :],
                                            iota_g[:, :, :].unsqueeze(1).to_broadcast([P, n, KEYS, GC]),
                                            in_groups(key_rel, u, g, n, KEYS), ALU.is_equal).then_inc(hots_made, 1)
                    pipeline(dve, T, 4, 2, stage)

                @block.tensor
                def _(pe):
                    def degrees(t, u):
                        pe.wait_ge(win_out, (t + 1) * NG)
                        if late(t, 2):
                            pe.wait_ge(deg_out, t - 1)
                        for s in range(T):
                            last = nc.tensor.matmul(deg_ps[u][:, 0:1], strip[:, u, s, :], ones_h[:, :], start=s == 0, stop=s == T - 1)
                        last.then_inc(deg_made, 1)

                    def stage(k, u):
                        if is_tile(k):
                            for g in range(NG):
                                if g == 0:
                                    pe.wait_ge(src_made, k + 1)
                                if g % 2 == 0:
                                    pe.wait_ge(hots_made, k * PAIRS + g // 2 + 1)
                                b = (u * NG + g) % 2
                                if g >= 2 or late(k, 1):
                                    pe.wait_ge(win_out, k * NG + g - 1)
                                for j in range(GW):
                                    for c in range(WC):
                                        last = nc.tensor.matmul(win_ps[b][:, j, 0:KEYS], hot_src[:, u, g, :, j * WC + c],
                                                                hot_key[:, g, :, j * WC + c], start=c == 0, stop=c == WC - 1)
                                last.then_inc(win_done, 1)
                                if g == 2 and is_tile(k - 1) and late(k, 1):
                                    degrees(k - 1, 1 - u)
                                if g == 5:
                                    pe.wait_ge(x_made, k + 1)
                                    if late(k, 1):
                                        pe.wait_ge(xt_copied, k)
                                    for c in range(KC):
                                        last = nc.tensor.transpose(xt_ps[:, c * P:(c + 1) * P],
                                                                   xr[:, u, c * P:(c + 1) * P], ident[:, :])
                                    last.then_inc(x_turned, 1)
                        elif k == T:
                            degrees(k - 1, 1 - u)
                        t = k - 2
                        if is_tile(t):
                            pe.wait_ge(xt_copied, t + 1)
                            if late(t, 1):
                                pe.wait_ge(lo_made, t)
                            for c in range(KC):
                                last = nc.tensor.matmul(h_ps[:, 0:D], xt[:, u, c, :], w_gnn[:, 0, c, :],
                                                        start=c == 0, stop=c == KC - 1)
                            last.then_inc(prod, 1)
                    pipeline(pe, T, 4, 2, stage)

                @block.scalar
                def _(act):
                    def deg_copy(t, u):
                        act.wait_ge(deg_made, t + 1)
                        nc.scalar.activation(degs[:, bass.ds(t, 1)], deg_ps[u][:, 0:1], ACT.Copy).then_inc(deg_out, 1)

                    def stage(k, u):
                        t = k - 3
                        if is_tile(t):
                            act.wait_ge(prod, t + 1)
                            act.wait_ge(tile_scale, t + 1)
                            nc.scalar.activation(row(h_split, t)[:, 0:D], h_ps[:, 0:D], ACT.Copy,
                                                 scale=scale_up[:, 0, bass.ds(t, 1)]).then_inc(hi_made, 1)
                        if is_tile(k):
                            for g in range(NG):
                                if g == 0 and late(k, 2):
                                    act.wait_ge(deg_made, k - 1)
                                    act.wait_ge(strip_stored[u], (k - u) * 8)
                                act.wait_ge(win_done, k * NG + g + 1)
                                b = (u * NG + g) % 2
                                first, full, part = g * GW * WIN, GW, 0
                                if first + GW * WIN > P:
                                    full, part = divmod(P - first, WIN)
                                last = nc.scalar.activation(
                                    strip[:, u, :, first:first + full * WIN].rearrange("p s (j d) -> p j d s", d=WIN),
                                    win_ps[b][:, 0:full, 0:KEYS].rearrange("p j (d s) -> p j d s", d=WIN), ACT.Copy)
                                if part:
                                    last = nc.scalar.activation(
                                        strip[:, u, :, P - part:P].rearrange("p s d -> p d s"),
                                        win_ps[b][:, full, 0:part * T].rearrange("p (d s) -> p d s", d=part), ACT.Copy)
                                last.then_inc(win_out, 1)
                                if g == 6 and is_tile(k - 1) and late(k, 1):
                                    deg_copy(k - 1, 1 - u)
                            act.wait_ge(x_turned, k + 1)
                            if late(k, 2):
                                act.wait_ge(prod, k - 1)
                            nc.scalar.activation(xt[:, u, :, :].rearrange("p c n -> p (c n)"), xt_ps[:, 0:D],
                                                 ACT.Copy).then_inc(xt_copied, 1)
                            act.wait_ge(win_out, (k + 1) * NG)
                            act.dma_start(count_tab[bass.ds(k, 1), :, :].rearrange("a p m -> p (a m)"),
                                          strip[:, u, :, :].rearrange("p s d -> p (s d)")).then_inc(strip_stored[u], 16)
                        elif k == T:
                            deg_copy(k - 1, 1 - u)
                    pipeline(act, T, 4, 2, stage)

        total_made, total_done, flag_made = (sem(s) for s in ("total_made", "total_done", "flag_made"))
        with ExitStack() as ph:
            part_sum = sb(ph, "part_sum", [P, 1])
            total_ps = ps(ph, "total_ps", [P, 1])
            with nc.Block() as block:
                @block.vector
                def _(dve):
                    nc.vector.tensor_reduce(part_sum[:, :], degs[:, :], AX.X, ALU.add).then_inc(total_made, 1)
                    dve.wait_ge(total_done, 1)
                    nc.vector.tensor_scalar(flag[:, :], total_ps[0:1, :], float(E), None, ALU.is_equal).then_inc(flag_made, 1)

                @block.tensor
                def _(pe):
                    pe.wait_ge(total_made, 1)
                    nc.tensor.matmul(total_ps[:, :], ones_f[:, :], part_sum[:, :], start=True, stop=True).then_inc(total_done, 1)

        strips = sb(h_stack, "strips", [P, RING, T * P], F16)
        half_strip = T * P // 2
        assert CH <= half_strip
        dst_col = strips[:, 0, :].bitcast(F32)[:, 0:CH]
        src_col = strips[:, 1, :].bitcast(I32)[:, 0:CH]
        tab = sb(h_stack, "tab", [1, T, 4], I32)

        U = 8
        g_loaded, g_turned, g_out, split_done, onehots_ready, onehots_used, deg_done = (
            sem(s) for s in ("g_loaded", "g_turned", "g_out", "split_done", "onehots_ready", "onehots_used", "deg_done"))
        rows_loaded, rng, tab_stored, tab_loaded, cnt_ready, kdown_set = (
            sem(s) for s in ("rows_loaded", "rng", "tab_stored", "tab_loaded", "cnt_ready", "kdown_set"))
        with ExitStack() as ph:
            nat = sb(ph, "nat", [P, 2, P])
            part_i = strips[:, 2, :].bitcast(I32)[:, 0:CH]
            dst_i = strips[:, 3, :].bitcast(I32)[:, 0:CH]
            row_f = h_split[:, :, :].rearrange("p t d -> p (t d)")[:, 0:2 * CH].bitcast(F32)
            tile_f = h_split[:, :, :].rearrange("p t d -> p (t d)")[:, 2 * CH:4 * CH].bitcast(F32)
            zero_h = sb(ph, "zero_h", [P, P], F16)
            hot_row = sb(ph, "hot_row", [P, U, P], F16)
            hot_tile = sb(ph, "hot_tile", [P, U, T], F16)
            tr = [ps(ph, f"tr{i}", [P, 512]) for i in range(2)]
            deg_ps = ps(ph, "gdeg_ps", [P, T])
            with nc.Block() as block:
                @block.sync
                def _(sp):
                    with sp.If(counted(sp) == 0):
                        for b in range(CB):
                            if b >= 1:
                                sp.wait_ge(g_turned, 2 * b)
                            sp.dma_start(nat[:, 0, :], dst_tab[b * P:(b + 1) * P, :]).then_inc(g_loaded, 16)
                            sp.dma_start(nat[:, 1, :], src_tab[b * P:(b + 1) * P, :]).then_inc(g_loaded, 16)

                @block.tensor
                def _(pe):
                    with pe.If(counted(pe) == 0):
                        for b in range(CB):
                            pe.wait_ge(g_loaded, 32 * (b + 1))
                            if b >= 1:
                                pe.wait_ge(g_out, 2 * b)
                            for i in range(2):
                                nc.tensor.transpose(tr[i][:, 0:P], nat[:, i, :], ident[:, :]).then_inc(g_turned, 1)
                        pe.wait_ge(split_done, 1)
                        nc.tensor.matmul(deg_ps[:, :], zero_h[:, :], zero_h[:, 0:T], start=True, stop=False)
                        with pe.Fori(0, CH // U) as it:
                            for u in range(U):
                                pe.wait_ge(onehots_ready, it * U + u + 1)
                                nc.tensor.matmul(deg_ps[:, :], hot_row[:, u, :], hot_tile[:, u, :], start=False,
                                                 stop=False).then_inc(onehots_used, 1)
                        nc.tensor.matmul(deg_ps[:, :], zero_h[:, :], zero_h[:, 0:T], start=False, stop=True).then_inc(deg_done, 1)

                @block.vector
                def _(dve):
                    v = nc.vector
                    with dve.If(counted(dve) == 0):
                        v.memset(zero_h[:, :], 0.0).then_inc(split_done, 1)
                        for b in range(CB):
                            dve.wait_ge(g_turned, 2 * b + 2)
                            v.tensor_copy(dst_col[:, b * P:(b + 1) * P], tr[0][:, 0:P]).then_inc(g_out, 1)
                            v.tensor_copy(src_col[:, b * P:(b + 1) * P], tr[1][:, 0:P]).then_inc(g_out, 1)
                        dve.wait_ge(g_out, 2 * CB)
                        v.tensor_copy(dst_i, dst_col).then_inc(split_done, 1)
                        dve.wait_ge(split_done, 2)
                        v.tensor_scalar(part_i, dst_i, P - 1, None, ALU.bitwise_and).then_inc(split_done, 1)
                        dve.wait_ge(split_done, 3)
                        v.tensor_copy(row_f, part_i).then_inc(split_done, 1)
                        dve.wait_ge(split_done, 4)
                        v.tensor_scalar(part_i, dst_i, P.bit_length() - 1, None, ALU.arith_shift_right).then_inc(split_done, 1)
                        dve.wait_ge(split_done, 5)
                        v.tensor_copy(tile_f, part_i).then_inc(split_done, 1)
                        dve.wait_ge(split_done, 6)

                        def chunks(it, first):
                            for u in range(U):
                                k = it * U + u
                                if not first:
                                    dve.wait_ge(onehots_used, (it - 1) * U + u + 1)
                                v.tensor_scalar(hot_row[:, u, :], iota_h[:, 0:P], row_f[:, bass.ds(k, 1)], None, ALU.is_equal)
                                v.tensor_scalar(hot_tile[:, u, :], iota_h[:, 0:T], tile_f[:, bass.ds(k, 1)], None,
                                                ALU.is_equal).then_inc(onehots_ready, 1)
                        chunks(0, True)
                        with dve.Fori(1, CH // U) as it:
                            chunks(it, False)
                        dve.wait_ge(deg_done, 1)
                        v.tensor_copy(degs[:, :], deg_ps[:, :]).then_inc(split_done, 1)

        with ExitStack() as ph:
            least = sb(ph, "least", [P, CH])
            most = sb(ph, "most_b", [P, CH])
            kup = strips[:, 2, :].bitcast(F32)[:, 0:CH]
            kdown = strips[:, 3, :].bitcast(F32)[:, 0:CH]
            thr = sb(ph, "thr_t", [P, 2])
            ends = sb(ph, "ends", [P, 4])
            pair = sb(ph, "pair", [P, 2])
            line = sb(ph, "line", [1, T, 2])
            cum = sb(ph, "cum", [1, T])
            zline = sb(ph, "zline", [1, T])
            tab_f = sb(ph, "tab_f", [1, T, 4])
            with nc.Block() as block:
                @block.sync
                def _(sp):
                    with sp.If(counted(sp) == 0):
                        sp.dma_start(least[:, :], least_tab.rearrange("b p -> (b p)").partition_broadcast(P)).then_inc(rows_loaded, 16)
                        sp.dma_start(most[:, :], most_tab.rearrange("b p -> (b p)").partition_broadcast(P)).then_inc(rows_loaded, 16)
                        sp.wait_ge(cnt_ready, 1)
                        sp.dma_start(range_tab[:, :], pair[0:T, :]).then_inc(tab_stored, 16)
                        sp.wait_ge(tab_stored, 16)
                        sp.dma_start(line[:, :, :], range_tab.rearrange("(a t) c -> a t c", a=1)).then_inc(tab_loaded, 16)
                        sp.wait_ge(tab_loaded, 16)

                @block.gpsimd
                def _(pool):
                    with pool.If(counted(pool) == 0):
                        nc.gpsimd.iota(kup, [[1, CH]], base=1, channel_multiplier=0,
                                       allow_small_or_imprecise_dtypes=True)
                        nc.gpsimd.iota(kdown, [[-1, CH]], base=CH, channel_multiplier=0,
                                       allow_small_or_imprecise_dtypes=True).then_inc(kdown_set, 1)

                @block.vector
                def _(dve):
                    n = [0]

                    def link(ins):
                        n[0] += 1
                        ins.then_inc(rng, 1)
                        dve.wait_ge(rng, n[0])
                    v = nc.vector
                    with dve.If(counted(dve) == 0):
                        v.tensor_scalar(thr[:, 0:1], iota_part[:, :], float(P), None, ALU.mult)
                        link(v.tensor_scalar(thr[:, 1:2], iota_part[:, :], float(P), float(P - 1), ALU.mult, ALU.add))
                        dve.wait_ge(rows_loaded, 32)
                        dve.wait_ge(kdown_set, 1)
                        link(v.scalar_tensor_tensor(most[:, :], most[:, :], thr[:, 0:1], kdown, ALU.is_ge, ALU.mult))
                        link(v.scalar_tensor_tensor(least[:, :], least[:, :], thr[:, 1:2], kup, ALU.is_le, ALU.mult))
                        link(v.tensor_reduce(ends[:, 0:1], most[:, :], AX.X, ALU.max))
                        link(v.tensor_reduce(ends[:, 1:2], least[:, :], AX.X, ALU.max))
                        link(v.tensor_scalar(pair[:, 0:1], ends[:, 0:1], -1.0, float(CH), ALU.mult, ALU.add))
                        link(v.tensor_tensor(ends[:, 2:3], ends[:, 1:2], pair[:, 0:1], ALU.subtract))
                        v.tensor_scalar(pair[:, 1:2], ends[:, 2:3], 1.0, None, ALU.max).then_inc(cnt_ready, 1)
                        link(v.memset(zline[:, :], 0.0))
                        dve.wait_ge(tab_loaded, 16)
                        link(v.tensor_tensor_scan(cum[:, :], line[:, :, 1], zline[:, :], 0.0, ALU.add, ALU.add))
                        link(v.tensor_tensor(tab_f[:, :, 0], cum[:, :], line[:, :, 1], ALU.subtract))
                        v.tensor_copy(tab_f[:, :, 1], line[:, :, 1])
                        v.tensor_copy(tab_f[:, :, 3], line[:, :, 1])
                        link(v.tensor_copy(tab_f[:, :, 2], line[:, :, 0]))
                        link(v.tensor_copy(tab[:, :, :], tab_f[:, :, :]))

        deg1_made, dinv_made = sem("deg1_made"), sem("dinv_made")
        with nc.Block() as block:
            @block.vector
            def _(dve):
                with only(dve, False):
                    nc.vector.tensor_scalar(degs[:, :], degs[:, :], 1.0, None, ALU.add).then_inc(deg1_made, 1)
                    dve.wait_ge(dinv_made, 1)
                for i in range(L):
                    nc.vector.tensor_scalar(scale_up[:, i, :], dinv[:, :], sigma[:, i, 0:1], None, ALU.mult)
                    nc.vector.tensor_scalar(scale_down[:, i, :], dinv[:, :], sigma[:, i, 1:2], None, ALU.mult)

            @block.gpsimd
            def _(pool):
                with only(pool, False):
                    pool.wait_ge(deg1_made, 1)
                    nc.gpsimd.tensor_tensor(dinv[:, :], degs[:, :], neg_half[:, :], ALU.pow).then_inc(dinv_made, 1)


        def layer_input(dve, i, t, xr, dch, base):
            v = nc.vector
            tt = bass.ds(t, 1)
            v.tensor_scalar(xr, row(state, t), mv[:, tt, 0:1].rearrange("p a c -> p (a c)"), rstd[:, tt],
                            ALU.subtract, ALU.mult).then_inc(dch, 1)
            if i > 0:
                dve.wait_ge(dch, base + 1)
                v.tensor_tensor(xr, xr, rows3[:, i - 1, 1, :], ALU.mult).then_inc(dch, 1)
                dve.wait_ge(dch, base + 2)
                v.tensor_tensor(xr, xr, rows3[:, i - 1, 2, :], ALU.add).then_inc(dch, 1)
                dve.wait_ge(dch, base + 3)
                v.tensor_scalar(xr, xr, 0.0, None, ALU.max).then_inc(dch, 1)

        def layer_product(i):
            nm = f"l{i}p"
            per = 1 if i == 0 else 4
            b = (i + 1) * T
            bd = 0 if i == 0 else T + (i - 1) * T * per
            with ExitStack() as ph:
                xr = sb(ph, f"{nm}_xr", [P, 2, D])
                xt = sb(ph, f"{nm}_xt", [P, 2, KC, P])
                xt_ps = ps(ph, f"{nm}_xt_ps", [P, 2, 512])
                h_ps = ps(ph, f"{nm}_h_ps", [P, 2, 512])
                with nc.Block() as block:
                    def is_tile(t):
                        return not isinstance(t, int) or 0 <= t < T

                    def late(t, n):
                        return not isinstance(t, int) or t >= n

                    @block.vector
                    def _(dve):
                        with only(dve, False):
                            def stage(k, u):
                                if is_tile(k):
                                    if late(k, 2):
                                        dve.wait_ge(x_turned, b + k - 1)
                                    layer_input(dve, i, k, xr[:, u, :], dch, bd + k * per)
                                    dve.wait_ge(dch, bd + (k + 1) * per)
                                    dve.sem_inc(x_made, 1)
                                t = k - 2
                                if is_tile(t) and late(k, 2):
                                    dve.wait_ge(hi_made, b + t + 1)
                                    nc.vector.scalar_tensor_tensor(row(h_split, t)[:, D:2 * D], h_ps[:, u, 0:D],
                                                                   scale_up[:, i, bass.ds(t, 1)], row(h_split, t)[:, 0:D],
                                                                   ALU.mult, ALU.subtract).then_inc(lo_made, 1)
                            pipeline(dve, T, 2, 2, stage)

                    @block.tensor
                    def _(pe):
                        with only(pe, False):
                            def stage(k, u):
                                if is_tile(k):
                                    pe.wait_ge(x_made, b + k + 1)
                                    if late(k, 2):
                                        pe.wait_ge(xt_copied, b + k - 1)
                                    for c in range(KC):
                                        last = nc.tensor.transpose(xt_ps[:, u, c * P:(c + 1) * P],
                                                                   xr[:, u, c * P:(c + 1) * P], ident[:, :])
                                    last.then_inc(x_turned, 1)
                                t = k - 1
                                if is_tile(t):
                                    pe.wait_ge(xt_copied, b + t + 1)
                                    if late(k, 4):
                                        pe.wait_ge(lo_made, b + t - 1)
                                    for c in range(KC):
                                        last = nc.tensor.matmul(h_ps[:, 1 - u, 0:D], xt[:, 1 - u, c, :], w_gnn[:, i, c, :],
                                                                start=c == 0, stop=c == KC - 1)
                                    last.then_inc(prod, 1)
                            pipeline(pe, T, 4, 2, stage)

                    @block.scalar
                    def _(act):
                        with only(act, False):
                            def stage(k, u):
                                if is_tile(k):
                                    act.wait_ge(x_turned, b + k + 1)
                                    if late(k, 2):
                                        act.wait_ge(prod, b + k - 1)
                                    nc.scalar.activation(xt[:, u, :, :].rearrange("p c n -> p (c n)"), xt_ps[:, u, 0:D],
                                                         ACT.Copy).then_inc(xt_copied, 1)
                                t = k - 1
                                if is_tile(t):
                                    act.wait_ge(prod, b + t + 1)
                                    nc.scalar.activation(row(h_split, t)[:, 0:D], h_ps[:, 1 - u, 0:D], ACT.Copy,
                                                         scale=scale_up[:, i, bass.ds(t, 1)]).then_inc(hi_made, 1)
                            pipeline(act, T, 2, 2, stage)

        def await_slot(eng, s, i, t, n):
            if not isinstance(t, int) or t >= n:
                eng.wait_ge(s, i * T + t - n + 1)
            elif i > 0:
                eng.wait_ge(s, i * T - (T - 1 - t) % n)

        def counted_layers():
            h_ab = (h_split[:, :, :], state[:, :, :].bitcast(F16))
            c_loaded = [sem(f"c_loaded{r}") for r in range(RING)]
            strip_done, low_out, both, biased, seen, stat_ch, tile_rstd = (
                sem(s) for s in ("strip_done", "low_out", "both", "biased", "seen", "stat_ch", "tile_rstd"))
            x_in_loaded = [sem(f"x_in_loaded{u}") for u in range(2)]
            y_ch, own_made, own_added = sem("y_ch"), sem("own_made"), sem("own_added")
            loads = [len(range(r, T, RING)) for r in range(RING)]
            DEPTH = 4
            with ExitStack() as ph:
                low = sb(ph, "low", [P, 2, D])
                own = sb(ph, "own", [P, 2, D])
                total = sb(ph, "total", [P, 2, D])
                xr = sb(ph, "xr", [P, 2, D])
                xt = sb(ph, "xt", [P, 2, KC, P])
                x_in = sb(ph, "x_in", [P, 2, D])
                tiny = sb(ph, "tiny", [P, 4])
                acc = [ps(ph, f"acc{r}", [P, 512]) for r in range(RING)]
                xt_ps = ps(ph, "xt_ps", [P, 2, 512])
                h_ps = ps(ph, "h_ps_l", [P, 2, 512])

                def is_tile(t):
                    return not isinstance(t, int) or 0 <= t < T

                def stat(t, c):
                    return stats6[:, bass.ds(t, 1), c:c + 1].rearrange("p a c -> p (a c)")

                def mean(t):
                    return mv[:, bass.ds(t, 1), 0:1].rearrange("p a c -> p (a c)")

                def variance(t):
                    return mv[:, bass.ds(t, 1), 1:2].rearrange("p a c -> p (a c)")

                with nc.Block() as block:
                    @block.sync
                    def _(sp):
                        with sp.If(counted(sp) == 1):
                            for i in range(L):
                                def stage(t, r):
                                    if is_tile(t):
                                        await_slot(sp, strip_done, i, t, RING)
                                        sp.dma_start(strips[:, r, :],
                                                     count_tab[bass.ds(t, 1), :, :].rearrange("a p m -> p (a m)"))\
                                          .then_inc(c_loaded[r], 16)
                                pipeline(sp, T, RING, RING, stage)

                    @block.tensor
                    def _(pe):
                        with pe.If(counted(pe) == 1):
                            for i in range(L):
                                def sum_up(i, k, r, first, end):
                                    if first == 0:
                                        pe.wait_ge(c_loaded[r], i * loads[r] * 16 + (k - r) * (16 // RING) + 16)
                                        await_slot(pe, both, i, k, RING)
                                    for s in range(first, end):
                                        last = nc.tensor.matmul(acc[r][:, :], strips[:, r, s * P:(s + 1) * P],
                                                                h_ab[i % 2][:, s, :], start=s == 0, stop=s == T - 1)
                                    if end == T:
                                        last.then_inc(strip_done, 1)

                                def stage(k, r):
                                    if is_tile(k):
                                        ahead = i > 0 and isinstance(k, int) and k == 0
                                        sum_up(i, k, r, T - 3 if ahead else 0, T)
                                    if i == L - 1:
                                        return
                                    if isinstance(k, int) and k == T:
                                        pe.wait_ge(hi_made, (i + 2) * T - 3)
                                        pe.wait_ge(lo_made, (i + 2) * T - 3)
                                        sum_up(i + 1, 0, 0, 0, T - 3)
                                    t, u, n = k - 1, (r - 1) % 2, i + 1
                                    if is_tile(t):
                                        pe.wait_ge(xr_made, i * T + t + 1)
                                        await_slot(pe, xt_copied, n, t, 2)
                                        for c in range(KC):
                                            last = nc.tensor.transpose(xt_ps[:, u, c * P:(c + 1) * P],
                                                                       xr[:, u, c * P:(c + 1) * P], ident[:, :])
                                        last.then_inc(x_turned, 1)
                                    t, u = k - 2, r % 2
                                    if is_tile(t):
                                        pe.wait_ge(xt_copied, n * T + t + 1)
                                        await_slot(pe, lo_made, n, t, 2)
                                        for c in range(KC):
                                            last = nc.tensor.matmul(h_ps[:, u, 0:D], xt[:, u, c, :], w_gnn[:, n, c, :],
                                                                    start=c == 0, stop=c == KC - 1)
                                        last.then_inc(prod, 1)
                                pipeline(pe, T, DEPTH, RING, stage)
                                if i < L - 1:
                                    pe.wait_ge(hi_made, (i + 2) * T)
                                    pe.wait_ge(lo_made, (i + 2) * T)

                    @block.scalar
                    def _(act):
                        with act.If(counted(act) == 1):
                            for i in range(L):
                                h_out = h_ab[(i + 1) % 2]

                                def stage(k, r):
                                    if i == L - 1 and is_tile(k):
                                        if not isinstance(k, int) or k >= 2:
                                            act.wait_ge(y_ch, 4 * (k - 1))
                                        if isinstance(k, int) and k == T - 1:
                                            act.dma_start(x_in[0:LAST, r % 2, :], x[(T - 1) * P:N, :])\
                                               .then_inc(x_in_loaded[r % 2], 16)
                                        else:
                                            act.dma_start(x_in[:, r % 2, :], x[bass.ds(k * P, P), :])\
                                               .then_inc(x_in_loaded[r % 2], 16)
                                    if is_tile(k):
                                        act.wait_ge(strip_done, i * T + k + 1)
                                        await_slot(act, both, i, k, 2)
                                        nc.scalar.activation(low[:, r % 2, :], acc[r][:, D:2 * D], ACT.Copy).then_inc(low_out, 1)
                                    if i == L - 1:
                                        return
                                    t, u, n = k - 1, (r - 1) % 2, i + 1
                                    if is_tile(t):
                                        act.wait_ge(x_turned, n * T + t + 1)
                                        await_slot(act, prod, n, t, 2)
                                        for c in range(KC):
                                            last = nc.scalar.activation(xt[:, u, c, :], xt_ps[:, u, c * P:(c + 1) * P],
                                                                        ACT.Relu, scale=cols2[:, i, 0, c:c + 1],
                                                                        bias=cols2[:, i, 1, c:c + 1])
                                        last.then_inc(xt_copied, 1)
                                    t, u = k - 2, r % 2
                                    if is_tile(t):
                                        act.wait_ge(prod, n * T + t + 1)
                                        nc.scalar.activation(row(h_out, t)[:, 0:D], h_ps[:, u, 0:D], ACT.Copy,
                                                             scale=scale_up[:, n, bass.ds(t, 1)]).then_inc(hi_made, 1)
                                pipeline(act, T, DEPTH, RING, stage)

                    @block.vector
                    def _(dve):
                        v = nc.vector

                        def statistics(base, t):
                            dve.wait_ge(stat_ch, base + 1)
                            v.tensor_tensor(tiny[:, 0:1], stat(t, 1), stat(t, 4), ALU.subtract).then_inc(stat_ch, 1)
                            v.scalar_tensor_tensor(tiny[:, 1:2], stat(t, 2), D * EPS, stat(t, 5), ALU.add, ALU.add)\
                             .then_inc(stat_ch, 1)
                            dve.wait_ge(stat_ch, base + 3)
                            v.scalar_tensor_tensor(mean(t), tiny[:, 0:1], -0.5, stat(t, 1), ALU.mult, ALU.add)\
                             .then_inc(stat_ch, 1)
                            v.scalar_tensor_tensor(tiny[:, 2:3], tiny[:, 0:1], 0.25, tiny[:, 0:1], ALU.mult, ALU.mult)\
                             .then_inc(stat_ch, 1)
                            dve.wait_ge(stat_ch, base + 5)
                            v.scalar_tensor_tensor(variance(t), tiny[:, 1:2], 1.0 / D, tiny[:, 2:3], ALU.mult, ALU.add)\
                             .then_inc(stat_ch, 1)

                        with dve.If(counted(dve) == 1):
                            for i in range(L):
                                h_out = h_ab[(i + 1) % 2]

                                def stage(k, r):
                                    u = r % 2
                                    if is_tile(k):
                                        g = i * T + k
                                        dve.wait_ge(own_added, g + 1)
                                        v.tensor_tensor(total[:, u, :], acc[r][:, 0:D], low[:, u, :], ALU.add).then_inc(both, 1)
                                        dve.wait_ge(both, g + 1)
                                        v.scalar_tensor_tensor(total[:, u, :], total[:, u, :], scale_down[:, i, bass.ds(k, 1)],
                                                               rows3[:, i, 0, :], ALU.mult, ALU.add).then_inc(biased, 1)
                                        dve.wait_ge(biased, g + 1)
                                        dve.sem_inc(seen, 1)
                                        v.bn_stats(row(stats6, k), total[:, u, :]).then_inc(stat_ch, 1)
                                        statistics(g * 6, k)
                                        dve.wait_ge(tile_rstd, g + 1)
                                        if i < L - 1:
                                            await_slot(dve, x_turned, i + 1, k, 2)
                                        v.tensor_scalar(xr[:, u, :], total[:, u, :], mean(k), rstd[:, bass.ds(k, 1)],
                                                        ALU.subtract, ALU.mult).then_inc(xr_made, 1)
                                        if i == L - 1:
                                            dve.wait_ge(xr_made, g + 1)
                                            v.tensor_tensor(xr[:, u, :], xr[:, u, :], rows3[:, i, 1, :], ALU.mult).then_inc(y_ch, 1)
                                            dve.wait_ge(y_ch, 4 * k + 1)
                                            v.tensor_tensor(xr[:, u, :], xr[:, u, :], rows3[:, i, 2, :], ALU.add).then_inc(y_ch, 1)
                                            dve.wait_ge(y_ch, 4 * k + 2)
                                            dve.wait_ge(x_in_loaded[u], (k - u) * 8 + 16)
                                            v.scalar_tensor_tensor(row(state, k), xr[:, u, :], 0.0, x_in[:, u, :],
                                                                   ALU.max, ALU.add).then_inc(y_ch, 1)
                                            dve.wait_ge(y_ch, 4 * k + 3)
                                            dve.sem_inc(y_ch, 1)
                                            v.bn_stats(row(stats6, k), row(state, k))
                                    t, n = k - 2, i + 1
                                    if i < L - 1 and is_tile(t):
                                        dve.wait_ge(hi_made, n * T + t + 1)
                                        v.scalar_tensor_tensor(row(h_out, t)[:, D:2 * D], h_ps[:, u, 0:D],
                                                               scale_up[:, n, bass.ds(t, 1)], row(h_out, t)[:, 0:D],
                                                               ALU.mult, ALU.subtract).then_inc(lo_made, 1)
                                pipeline(dve, T, DEPTH, RING, stage)

                    @block.gpsimd
                    def _(pool):
                        with pool.If(counted(pool) == 1):
                            for i in range(L):
                                if i > 0:
                                    pool.wait_ge(hi_made, (i + 1) * T)
                                    pool.wait_ge(lo_made, (i + 1) * T)
                                h_in = h_ab[i % 2]

                                def stage(t, r):
                                    if is_tile(t):
                                        u, g = r % 2, i * T + t
                                        await_slot(pool, own_added, i, t, 2)
                                        nc.gpsimd.tensor_tensor(own[:, u, :], row(h_in, t)[:, 0:D], row(h_in, t)[:, D:2 * D],
                                                                ALU.add).then_inc(own_made, 1)
                                        pool.wait_ge(own_made, g + 1)
                                        pool.wait_ge(low_out, g + 1)
                                        nc.gpsimd.tensor_tensor(low[:, u, :], low[:, u, :], own[:, u, :], ALU.add).then_inc(own_added, 1)
                                        pool.wait_ge(stat_ch, (i * T + t + 1) * 6)
                                        nc.gpsimd.tensor_tensor(rstd[:, bass.ds(t, 1)], variance(t), neg_half[:, 0:1],
                                                                ALU.pow).then_inc(tile_rstd, 1)
                                pipeline(pool, T, DEPTH, RING, stage)

        def layer_sum(i):
            nm = f"l{i}s"
            whole_made, h_stored, idx_ready, idx_seen, rows_ready, hot_ready, summed, free, iota_set, g_biased = (
                sem(f"{nm}_{s}") for s in ("whole", "h_stored", "idx", "idx_seen", "rows", "hot", "summed", "free", "iota", "g_biased"))
            with ExitStack() as ph:
                idx = sb(ph, f"{nm}_idx", [P, 1], I32)
                rows = sb(ph, f"{nm}_rows", [P, D])
                hot = sb(ph, f"{nm}_hot", [P, P])
                tile_iota = sb(ph, f"{nm}_iota_t", [P, P])
                sum_ps = ps(ph, f"{nm}_ps", [P, D])

                def entry(eng, t, c, least, most):
                    return eng.value_load(tab[0:1, bass.ds(t, 1), c:c + 1].rearrange("p a b -> p (a b)"),
                                          min_val=least, max_val=most)

                def steps(eng, body, tail=None):
                    with eng.Fori(0, T) as t:
                        s0 = entry(eng, t, 0, 0, T * CH)
                        n = entry(eng, t, 1, 1, CH)
                        k0 = entry(eng, t, 2, 0, CH - 1)
                        with eng.Fori(0, n) as j:
                            body(t, s0 + j, k0 + j)
                        if tail:
                            tail(t)

                with nc.Block() as block:
                    @block.sync
                    def _(sp):
                        with sp.If(counted(sp) == 0):
                            with sp.Fori(0, T) as t:
                                sp.wait_ge(whole_made, t + 1)
                                sp.dma_start(h_tab[bass.ds(t * P, P), :], row(state, t)).then_inc(h_stored, 16)

                    @block.tensor
                    def _(pe):
                        with pe.If(counted(pe) == 0):
                            def body(t, s, k):
                                pe.wait_ge(rows_ready, (s + 1) * 16)
                                pe.wait_ge(hot_ready, s + 1)
                                pe.wait_ge(free, s + 1)
                                nc.tensor.matmul(sum_ps[:, :], hot[:, :], rows[:, :], start=True, stop=True).then_inc(summed, 1)
                            steps(pe, body)

                    @block.vector
                    def _(dve):
                        v = nc.vector
                        with dve.If(counted(dve) == 0):
                            with dve.Fori(0, T) as t:
                                v.tensor_tensor(row(state, t), row(h_split, t)[:, 0:D], row(h_split, t)[:, D:2 * D],
                                                ALU.add).then_inc(whole_made, 1)
                            dve.wait_ge(whole_made, T)
                            dve.wait_ge(h_stored, 16 * T)
                            dve.sem_inc(free, 1)
                            v.tensor_copy(tile_iota[:, :], iota_row[:, :]).then_inc(iota_set, 1)
                            dve.wait_ge(iota_set, 1)

                            def body(t, s, k):
                                kk = nc.s_assert_within(k, 0, CH - 1)
                                v.tensor_scalar(hot[:, :], tile_iota[:, :], dst_col[:, bass.ds(kk, 1)], None,
                                                ALU.is_equal).then_inc(hot_ready, 1)
                                dve.wait_ge(summed, s + 1)
                                v.tensor_tensor(row(state, t), sum_ps[:, :], row(state, t), ALU.add).then_inc(free, 1)
                                dve.wait_ge(free, s + 2)

                            def tail(t):
                                v.tensor_scalar(tile_iota[:, :], tile_iota[:, :], float(P), None, ALU.add).then_inc(iota_set, 1)
                                dve.wait_ge(iota_set, t + 2)
                            steps(dve, body, tail)
                            with dve.Fori(0, T) as t:
                                v.scalar_tensor_tensor(row(state, t), row(state, t), scale_down[:, i, bass.ds(t, 1)],
                                                       rows3[:, i, 0, :], ALU.mult, ALU.add).then_inc(g_biased, 1)
                            dve.wait_ge(g_biased, T)
                            with dve.Fori(0, T) as t:
                                v.bn_stats(row(stats6, t), row(state, t))

                    @block.gpsimd
                    def _(pool):
                        with pool.If(counted(pool) == 0):
                            pool.wait_ge(h_stored, 16 * T)

                            def body(t, s, k):
                                kk = nc.s_assert_within(k, 0, CH - 1)
                                pool.wait_ge(free, s + 1)
                                nc.gpsimd.tensor_copy(idx[:, :], src_col[:, bass.ds(kk, 1)]).then_inc(idx_ready, 1)
                                pool.wait_ge(idx_ready, s + 1)
                                pool.sem_inc(idx_seen, 1)
                                nc.gpsimd.indirect_dma_start(rows[:, :], None, h_tab[:, :],
                                                             bass.IndirectOffsetOnAxis(idx[:, 0:1], 0)).then_inc(rows_ready, 16)
                            steps(pool, body)

        counted_layers()
        for i in range(L):
            layer_product(i)
            layer_sum(i)
            rstd_of_rows(f"l{i}", i, False)

        fin, x_again, x_zero = sem("fin"), sem("x_again"), sem("x_zero")
        with ExitStack() as ph:
            x_tile = sb(ph, "x_tile", [P, D])
            xr = sb(ph, "fin_x", [P, D])
            with nc.Block() as block:
                @block.sync
                def _(sp):
                    with sp.If(counted(sp) == 0):
                        with sp.Fori(0, T - 1) as t:
                            sp.wait_ge(x_zero, t + 1)
                            sp.dma_start(x_tile[:, :], x[bass.ds(t * P, P), :]).then_inc(x_again, 16)
                        sp.wait_ge(x_zero, T)
                        sp.dma_start(x_tile[0:LAST, :], x[(T - 1) * P:N, :]).then_inc(x_again, 16)

                @block.vector
                def _(dve):
                    with dve.If(counted(dve) == 0):
                        nc.vector.memset(x_tile[:, :], 0.0).then_inc(x_zero, 1)
                        with dve.Fori(0, T) as t:
                            layer_input(dve, L, t, xr[:, :], fin, t * 4)
                            dve.wait_ge(fin, t * 4 + 4)
                            dve.wait_ge(x_again, (t + 1) * 16)
                            nc.vector.tensor_tensor(row(state, t), x_tile[:, :], xr[:, :], ALU.add).then_inc(x_zero, 1)
                            dve.wait_ge(x_zero, t + 2)
                            dve.sem_inc(y_made, 1)
                            nc.vector.bn_stats(row(stats6, t), row(state, t))
        rstd_of_rows("y", 1)
        h_stack.close()

        resid = state
        scan_h = sb(root, "scan_h", [P, T, D])
        with nc.Block() as block:
            @block.vector
            def _(dve):
                for t in range(T):
                    nc.vector.tensor_scalar(scan_h[:, t, :], resid[:, t, :], mv[:, t, 0:1], rstd[:, t:t + 1],
                                            ALU.subtract, ALU.mult)

        S = N_ITERS * G
        SLOTS = 4
        POOL_SUMS = 4
        pool_sum, dve_sum, out_stored = sem("pool_sum"), sem("dve_sum"), sem("out_stored")
        BANKS = -(-TS // 2)
        assert BANKS == 4
        TURN_LAG, VAR_LAG, PE_LAG, H_LAG = 4, 3, 1, 5
        names = ("tanh_done", "h2_done", "sig_done", "z_done", "var_done", "rstd_done", "z_turned", "zt_copied",
                 "prod_done", "h_done", "var_ch")
        (tanh_done, h2_done, sig_done, z_done, var_done, rstd_done, z_turned, zt_copied, prod_done, h_done,
         var_ch) = (sem(s) for s in names)
        with ExitStack() as ph:
            h2 = sb(ph, "h2", [P, SLOTS, TS, D])
            z = sb(ph, "z", [P, SLOTS, TS, D])
            zt = sb(ph, "zt", [P, 2, TS * KC, P])
            zst = sb(ph, "zst", [P, TS, 6])
            zhalf = sb(ph, "zhalf", [P, TS])
            zsum = sb(ph, "zsum", [P, TS])
            zvar = sb(ph, "zvar", [P, 2, TS])
            zrs = sb(ph, "zrs", [P, SLOTS, TS])
            zt_ps = [ps(ph, f"zt_ps{j}", [P, 512]) for j in range(BANKS)]
            h_ps = [ps(ph, f"h_ps{j}", [P, 512]) for j in range(BANKS)]

            def tiles(j):
                return min(2, TS - 2 * j)

            def on(s):
                return not isinstance(s, int) or 0 <= s < S

            def late(s, n):
                return not isinstance(s, int) or s >= n

            with nc.Block() as block:
                def add_up(engine, g):
                    a = slice(g * TS, (g + 1) * TS)
                    return engine.tensor_tensor(scan_h[:, a, :], scan_h[:, a, :], resid[:, a, :], ALU.add)

                @block.scalar
                def _(act):
                    def turn_out(s, u, j):
                        act.wait_ge(z_turned, s * BANKS + j + 1)
                        if late(s, 2):
                            act.wait_ge(prod_done, (s - 2) * BANKS + j + 1)
                        n = tiles(j) * D
                        nc.scalar.activation(zt[:, u, 4 * j:4 * j + 2 * tiles(j), :].rearrange("p a b -> p (a b)"),
                                             zt_ps[j][:, 0:n], ACT.Copy).then_inc(zt_copied, 1)

                    def stage(k, u):
                        if on(k):
                            if late(k, G):
                                act.wait_ge(h_done, (k - G + 1) * BANKS)
                            if late(k, SLOTS):
                                act.wait_ge(z_done, k - SLOTS + 1)
                            g = k % G
                            nc.scalar.activation(h2[:, u, :, :], scan_h[:, bass.ds(g * TS, TS), :], ACT.Tanh).then_inc(tanh_done, 1)
                        s = k - TURN_LAG
                        if on(s):
                            for j in range(BANKS // 2):
                                turn_out(s, (u - TURN_LAG) % 2, j)
                        s = k - 2
                        if on(s):
                            act.wait_ge(h2_done, s + 1)
                            if late(s, SLOTS):
                                act.wait_ge(z_turned, (s - SLOTS + 1) * BANKS)
                                act.wait_ge(var_done, s - SLOTS + 1)
                            nc.scalar.activation(z[:, (u - 2) % SLOTS, :, :], h2[:, (u - 2) % SLOTS, :, :],
                                                 ACT.Sigmoid).then_inc(sig_done, 1)
                        s = k - TURN_LAG
                        if on(s):
                            for j in range(BANKS // 2, BANKS):
                                turn_out(s, (u - TURN_LAG) % 2, j)
                    pipeline(act, S, 8, SLOTS, stage)

                @block.vector
                def _(dve):
                    v = nc.vector

                    def stage(k, u):
                        s = k - 1
                        if on(s):
                            dve.wait_ge(tanh_done, s + 1)
                            w = (u - 1) % SLOTS
                            v.scalar_tensor_tensor(h2[:, w, :, :], h2[:, w, :, :], RES_SCALE,
                                                   scan_h[:, bass.ds((s % G) * TS, TS), :], ALU.mult, ALU.add).then_inc(h2_done, 1)
                        sv, sh = k - VAR_LAG, k - H_LAG

                        def h_bank(j):
                            if not on(sh):
                                return
                            dve.wait_ge(prod_done, sh * BANKS + j + 1)
                            for a in range(tiles(j)):
                                i = 2 * j + a
                                last = v.scalar_tensor_tensor(
                                    scan_h[:, bass.ds((sh % G) * TS + i, 1), :].rearrange("p a d -> p (a d)"),
                                    h_ps[j][:, a * D:(a + 1) * D], zrs[:, (u - H_LAG) % SLOTS, i:i + 1], b_scan[:, :],
                                    ALU.mult, ALU.add)
                            last.then_inc(h_done, 1)
                        if on(sh):
                            dve.wait_ge(rstd_done, sh + 1)
                        h_bank(0)
                        if on(sv):
                            dve.wait_ge(z_done, sv + 1)
                            for i in range(TS):
                                last = v.bn_stats(zst[:, i, :], z[:, (u - VAR_LAG) % SLOTS, i, :])
                            last.then_inc(var_ch, 1)
                        h_bank(1)
                        if on(sv):
                            dve.wait_ge(var_ch, sv * 4 + 1)
                            v.tensor_tensor(zhalf[:, :], zst[:, :, 1], zst[:, :, 4], ALU.subtract).then_inc(var_ch, 1)
                            v.scalar_tensor_tensor(zsum[:, :], zst[:, :, 2], D * EPS, zst[:, :, 5], ALU.add, ALU.add).then_inc(var_ch, 1)
                        h_bank(2)
                        if on(sv):
                            dve.wait_ge(var_ch, sv * 4 + 3)
                            v.scalar_tensor_tensor(zhalf[:, :], zhalf[:, :], 0.25, zhalf[:, :], ALU.mult, ALU.mult).then_inc(var_ch, 1)
                        h_bank(3)
                        if on(sv):
                            dve.wait_ge(var_ch, sv * 4 + 4)
                            if late(sv, 2):
                                dve.wait_ge(rstd_done, sv - 1)
                            v.scalar_tensor_tensor(zvar[:, (u - VAR_LAG) % 2, :], zsum[:, :], 1.0 / D, zhalf[:, :],
                                                   ALU.mult, ALU.add).then_inc(var_done, 1)
                    pipeline(dve, S, 8, SLOTS, stage)
                    dve.wait_ge(h_done, S * BANKS)
                    for g in range(POOL_SUMS, G):
                        add_up(v, g).then_inc(dve_sum, 1)

                @block.gpsimd
                def _(pool):
                    def stage(k, u):
                        if on(k):
                            pool.wait_ge(sig_done, k + 1)
                            nc.gpsimd.tensor_tensor(z[:, u, :, :], h2[:, u, :, :], z[:, u, :, :], ALU.mult).then_inc(z_done, 1)
                        s = k - 1
                        if on(s):
                            pool.wait_ge(var_done, s + 1)
                            w = (u - 1) % SLOTS
                            if late(s, SLOTS):
                                pool.wait_ge(h_done, (s - SLOTS + 1) * BANKS)
                            nc.gpsimd.tensor_tensor(zrs[:, w, :], zvar[:, w % 2, :], neg_half[:, 0:TS], ALU.pow).then_inc(rstd_done, 1)
                    pipeline(pool, S, 8, SLOTS, stage)
                    for g in range(POOL_SUMS):
                        pool.wait_ge(h_done, (S - G + g + 1) * BANKS)
                        add_up(nc.gpsimd, g).then_inc(pool_sum, 1)

                @block.tensor
                def _(pe):
                    def turn(s, u, j):
                        if late(s, 1):
                            pe.wait_ge(zt_copied, (s - 1) * BANKS + j + 1)
                        for a in range(tiles(j)):
                            for c in range(KC):
                                last = nc.tensor.transpose(zt_ps[j][:, (2 * a + c) * P:(2 * a + c + 1) * P],
                                                           z[:, u, 2 * j + a, c * P:(c + 1) * P], ident[:, :])
                        last.then_inc(z_turned, 1)

                    def multiply(s, u, j):
                        pe.wait_ge(zt_copied, s * BANKS + j + 1)
                        if late(s, 1):
                            pe.wait_ge(h_done, (s - 1) * BANKS + j + 1)
                        for a in range(tiles(j)):
                            for c in range(KC):
                                last = nc.tensor.matmul(h_ps[j][:, a * D:(a + 1) * D], zt[:, u, 4 * j + 2 * a + c, :],
                                                        w_scan[:, c, :], start=c == 0, stop=c == KC - 1)
                        last.then_inc(prod_done, 1)

                    def stage(k, u):
                        for j in range(BANKS):
                            if on(k):
                                if j == 0:
                                    pe.wait_ge(z_done, k + 1)
                                turn(k, u, j)
                            if on(k - PE_LAG):
                                multiply(k - PE_LAG, (u - PE_LAG) % 2, j)
                    pipeline(pe, S, 8, SLOTS, stage)

                @block.sync
                def _(sp):
                    for g in range(G):
                        if g < POOL_SUMS:
                            sp.wait_ge(pool_sum, g + 1)
                        else:
                            sp.wait_ge(dve_sum, g - POOL_SUMS + 1)
                        full = min((g + 1) * TS, T - 1)
                        sp.dma_start(out[g * TS * P:full * P, :].rearrange("(t p) d -> p t d", p=P),
                                     scan_h[:, g * TS:full, :]).then_inc(out_stored, 16)
                    sp.dma_start(out[(T - 1) * P:N, :], scan_h[0:LAST, T - 1, :]).then_inc(out_stored, 16)
                    sp.wait_ge(out_stored, 16 * (G + 1))


_INS = ["x", "src", "dst", "L0_gnn_W", "L0_gnn_b", "L0_gnn_gamma", "L0_gnn_beta",
        "L0_ffn_ln_w", "L0_ffn_ln_b", "L0_ffn_W", "L0_ffn_b"]


def kernel(**inputs):
    import numpy as _np
    import concourse.bacc as _bacc
    from concourse import mybir as _mybir
    from concourse.bass_utils import run_bass_kernel_spmd as _run

    nc = _bacc.Bacc("TRN2", target_bir_lowering=False, num_devices=1)
    arrays, args = {}, []
    for name in _INS:
        a = _np.ascontiguousarray(inputs[name])
        arrays[f"in_{name}_dram"] = a
        args.append(nc.dram_tensor(f"in_{name}_dram", a.shape, _mybir.dt.from_np(a.dtype), kind="ExternalInput").ap())
    shape = tuple(_np.shape(inputs["x"]))
    args.append(nc.dram_tensor("out_0_dram", shape, _mybir.dt.float32, kind="ExternalOutput").ap())
    build_gnn_ffn(nc, *args)
    r = _run(nc, [arrays], core_ids=[0])
    return r.results[0]["out_0_dram"]
```
